# Optimizing a Trainium2 kernel written in Bass

```python
import numpy as np
import jax
import jax.numpy as jnp

def _softmax(x, axis=-1):
    return jax.nn.softmax(x, axis=axis)

def _gelu(x):
    return jax.nn.gelu(x, approximate=True)

def _silu(x):
    return jax.nn.silu(x)

def _sigmoid(x):
    return jax.nn.sigmoid(x)

def _layernorm(x, axis=-1, eps=1e-05):
    m = jnp.mean(x, axis=axis, keepdims=True)
    v = jnp.var(x, axis=axis, keepdims=True)
    return (x - m) / jnp.sqrt(v + eps)

def _scatter_add(tgt, idx, src, axis=0):
    return tgt.at[idx].add(src)

def _segment_sum(src, seg, n):
    return jax.ops.segment_sum(src, seg, n)
kernel_name = 'mk_gnn_resnorm_d4_gnn_r64_c47192'

def setup_inputs(seed: int=0):
    np.random.seed(seed)
    _w = jnp.asarray

    def _rec_inputs():
        import jax
        import jax.numpy as jnp
        _gk = jax.random.key(seed)
        x = -0.0003713 + 1 * jax.random.normal(jax.random.fold_in(_gk, 1), (50000, 128), jnp.float32)
        src = jax.random.randint(jax.random.fold_in(_gk, 2), (12500,), 0, 50000, jnp.int32)
        dst = jax.random.randint(jax.random.fold_in(_gk, 3), (12500,), 0, 50000, jnp.int32)
        _o = jnp.argsort(dst, stable=True)
        src = src[_o]
        dst = dst[_o]
        edge_attr_64 = 0.000133148 + 1.00009 * jax.random.normal(jax.random.fold_in(_gk, 12), (12500, 64), jnp.float32)
        edge_type_3 = jax.random.randint(jax.random.fold_in(_gk, 14), (12500,), 0, 3, jnp.int32)
        edge_type_8 = jax.random.randint(jax.random.fold_in(_gk, 15), (12500,), 0, 8, jnp.int32)
        edge_weight = jax.random.uniform(jax.random.fold_in(_gk, 16), (12500,), jnp.float32, 0.0, 0.999999)
        node_type_3 = jax.random.randint(jax.random.fold_in(_gk, 17), (50000,), 0, 3, jnp.int32)
        return (x, src, dst, edge_attr_64, edge_type_3, edge_type_8, edge_weight, node_type_3)
    x, src, dst, edge_attr_64, edge_type_3, edge_type_8, edge_weight, node_type_3 = _rec_inputs()

    def _L0_gnn_setup():
        import jax, jax.numpy as jnp
        import numpy as np
        N = 100000
        E = 25000
        IN = 128
        H = 4
        C = 32
        ED = 64

        def _forward(x, edge_weight, edge_attr, Wq, Wk, Wv, We, gate, bias, src, dst):
            n = x.shape[0]
            q_s = (x @ Wq).reshape(n, H, C).sum(-1)
            k_s = (x @ Wk).reshape(n, H, C).sum(-1)
            v = (x @ Wv).reshape(n, H, C)
            e_s = edge_attr @ We.reshape(ED, H, C).sum(-1)
            inv_sqrt_c = 1.0 / jnp.sqrt(jnp.asarray(C, x.dtype))
            alpha = (q_s[dst] + k_s[src] + e_s) * inv_sqrt_c
            alpha = alpha + gate[None, :] * edge_weight[:, None]
            alpha = jnp.where(alpha >= 0, alpha, 0.2 * alpha)
            amax = jax.ops.segment_max(alpha, dst, num_segments=n)
            amax = jnp.where(jnp.isfinite(amax), amax, 0.0)
            ex = jnp.exp(alpha - amax[dst])
            denom = jax.ops.segment_sum(ex, dst, num_segments=n)
            attn = ex / (denom[dst] + 1e-16)
            msg = v[src] * attn[:, :, None]
            out = jax.ops.segment_sum(msg, dst, num_segments=n)
            return out.reshape(n, H * C) + bias
        key = jax.random.key(seed)
        ks = jax.random.split(key, 9)
        x = jax.random.normal(ks[0], (N, IN), jnp.float32)
        edge_index = jax.random.randint(ks[1], (2, E), 0, N, dtype=jnp.int32)
        edge_weight = jax.random.uniform(ks[2], (E,), jnp.float32)
        edge_attr = jax.random.normal(ks[3], (E, ED), jnp.float32)
        sq = float(np.sqrt(2.0 / (IN + H * C)))
        se = float(np.sqrt(2.0 / (ED + H * C)))
        Wq = jax.random.normal(ks[4], (IN, H * C), jnp.float32) * sq
        Wk = jax.random.normal(ks[5], (IN, H * C), jnp.float32) * sq
        Wv = jax.random.normal(ks[6], (IN, H * C), jnp.float32) * sq
        We = jax.random.normal(ks[7], (ED, H * C), jnp.float32) * se
        gate = jnp.ones((H,), jnp.float32)
        bias = jnp.zeros((H * C,), jnp.float32)
        return {'x': x, 'edge_index': edge_index, 'edge_weight': edge_weight, 'edge_attr': edge_attr, 'Wq': Wq, 'Wk': Wk, 'Wv': Wv, 'We': We, 'gate': gate, 'bias': bias}
    _L0_gnn_all = _L0_gnn_setup()
    _L0_gnn_in = {k: v for k, v in _L0_gnn_all.items() if k in ('Wq', 'Wk', 'Wv', 'We', 'gate', 'bias')}
    del _L0_gnn_all

    def _L1_gnn_setup():
        import jax, jax.numpy as jnp
        import numpy as np
        N, E, IN_DIM, HID, OUT = (50000, 9375, 128, 256, 128)
        key = jax.random.key(seed)
        k1, k2, k3, k4, k5, k6, k7 = jax.random.split(key, 7)
        h = jax.random.normal(k1, (N, IN_DIM), dtype=jnp.float32)
        src = jax.random.randint(k2, (E,), 0, N)
        dst = jax.random.randint(k3, (E,), 0, N)
        s1 = 1.0 / np.sqrt(2 * IN_DIM)
        s2 = 1.0 / np.sqrt(HID)
        W1 = jax.random.uniform(k4, (2 * IN_DIM, HID), minval=-s1, maxval=s1, dtype=jnp.float32)
        b1 = jax.random.uniform(k5, (HID,), minval=-s1, maxval=s1, dtype=jnp.float32)
        W2 = jax.random.uniform(k6, (HID, OUT), minval=-s2, maxval=s2, dtype=jnp.float32)
        b2 = jax.random.uniform(k7, (OUT,), minval=-s2, maxval=s2, dtype=jnp.float32)
        return {'h': h, 'src': src, 'dst': dst, 'W1': W1, 'b1': b1, 'W2': W2, 'b2': b2}
    _L1_gnn_all = _L1_gnn_setup()
    _L1_gnn_in = {k: v for k, v in _L1_gnn_all.items() if k in ('W1', 'b1', 'W2', 'b2')}
    del _L1_gnn_all

    def _L2_gnn_setup():
        import jax, jax.numpy as jnp
        import numpy as np
        N_NODES = 50000
        N_EDGES = 12500
        IN_FEAT = 128
        OUT_FEAT = 128
        NUM_REL = 8
        key = jax.random.key(seed)
        k_h, k_w, k_s, k_d, k_r = jax.random.split(key, 5)
        h = jax.random.normal(k_h, (N_NODES, IN_FEAT), dtype=jnp.float32)
        gain = float(np.sqrt(2.0))
        bound = gain * float(np.sqrt(6.0 / (IN_FEAT + OUT_FEAT)))
        weight = jax.random.uniform(k_w, (NUM_REL, IN_FEAT, OUT_FEAT), dtype=jnp.float32, minval=-bound, maxval=bound)
        src = jax.random.randint(k_s, (N_EDGES,), 0, N_NODES, dtype=jnp.int64)
        dst = jax.random.randint(k_d, (N_EDGES,), 0, N_NODES, dtype=jnp.int64)
        rel = jax.random.randint(k_r, (N_EDGES,), 0, NUM_REL, dtype=jnp.int64)
        return {'h': h, 'weight': weight, 'src': src, 'dst': dst, 'rel': rel}
    _L2_gnn_all = _L2_gnn_setup()
    _L2_gnn_in = {k: v for k, v in _L2_gnn_all.items() if k in ('weight',)}
    del _L2_gnn_all

    def _L3_gnn_setup():
        import jax, jax.numpy as jnp
        import numpy as np
        N_NODES = 50000
        N_EDGES = 12500
        D = 128
        T = 3
        NODE_IN = D + T * D
        key = jax.random.key(seed)
        ks = jax.random.split(key, 8)
        scale = 0.05
        return {'node_feature': jax.random.normal(ks[0], (N_NODES, D), jnp.float32), 'W_e': jax.random.normal(ks[1], (T, D, D), jnp.float32) * scale, 'b_e': jnp.zeros((T, D), jnp.float32), 'W_n': jax.random.normal(ks[2], (T, D, NODE_IN), jnp.float32) * scale, 'b_n': jnp.zeros((T, D), jnp.float32), 'edge_src': jax.random.randint(ks[3], (N_EDGES,), 0, N_NODES, jnp.int32), 'edge_dst': jax.random.randint(ks[4], (N_EDGES,), 0, N_NODES, jnp.int32), 'edge_type': jax.random.randint(ks[5], (N_EDGES,), 0, T, jnp.int32), 'node_type': jax.random.randint(ks[6], (N_NODES,), 0, T, jnp.int32)}
    _L3_gnn_all = _L3_gnn_setup()
    _L3_gnn_in = {k: v for k, v in _L3_gnn_all.items() if k in ('W_e', 'b_e', 'W_n', 'b_n')}
    del _L3_gnn_all
    return {'x': x, 'src': src, 'dst': dst, 'edge_attr_64': edge_attr_64, 'edge_type_3': edge_type_3, 'edge_type_8': edge_type_8, 'edge_weight': edge_weight, 'node_type_3': node_type_3, 'L0_gnn_Wq': _L0_gnn_in['Wq'], 'L0_gnn_Wk': _L0_gnn_in['Wk'], 'L0_gnn_Wv': _L0_gnn_in['Wv'], 'L0_gnn_We': _L0_gnn_in['We'], 'L0_gnn_gate': _L0_gnn_in['gate'], 'L0_gnn_bias': _L0_gnn_in['bias'], 'L1_gnn_W1': _L1_gnn_in['W1'], 'L1_gnn_b1': _L1_gnn_in['b1'], 'L1_gnn_W2': _L1_gnn_in['W2'], 'L1_gnn_b2': _L1_gnn_in['b2'], 'L2_gnn_weight': _L2_gnn_in['weight'], 'L3_gnn_W_e': _L3_gnn_in['W_e'], 'L3_gnn_b_e': _L3_gnn_in['b_e'], 'L3_gnn_W_n': _L3_gnn_in['W_n'], 'L3_gnn_b_n': _L3_gnn_in['b_n']}

def reference(x, src, dst, edge_attr_64, edge_type_3, edge_type_8, edge_weight, node_type_3, L0_gnn_Wq, L0_gnn_Wk, L0_gnn_Wv, L0_gnn_We, L0_gnn_gate, L0_gnn_bias, L1_gnn_W1, L1_gnn_b1, L1_gnn_W2, L1_gnn_b2, L2_gnn_weight, L3_gnn_W_e, L3_gnn_b_e, L3_gnn_W_n, L3_gnn_b_n):
    import jax
    import jax.numpy as jnp

    def _L0_gnn_ref(x, edge_index, edge_weight, edge_attr, Wq, Wk, Wv, We, gate, bias):
        import jax, jax.numpy as jnp
        import numpy as np
        N = 100000
        E = 25000
        IN = 128
        H = 4
        C = 32
        ED = 64

        def _forward(x, edge_weight, edge_attr, Wq, Wk, Wv, We, gate, bias, src, dst):
            n = x.shape[0]
            q_s = (x @ Wq).reshape(n, H, C).sum(-1)
            k_s = (x @ Wk).reshape(n, H, C).sum(-1)
            v = (x @ Wv).reshape(n, H, C)
            e_s = edge_attr @ We.reshape(ED, H, C).sum(-1)
            inv_sqrt_c = 1.0 / jnp.sqrt(jnp.asarray(C, x.dtype))
            alpha = (q_s[dst] + k_s[src] + e_s) * inv_sqrt_c
            alpha = alpha + gate[None, :] * edge_weight[:, None]
            alpha = jnp.where(alpha >= 0, alpha, 0.2 * alpha)
            amax = jax.ops.segment_max(alpha, dst, num_segments=n)
            amax = jnp.where(jnp.isfinite(amax), amax, 0.0)
            ex = jnp.exp(alpha - amax[dst])
            denom = jax.ops.segment_sum(ex, dst, num_segments=n)
            attn = ex / (denom[dst] + 1e-16)
            msg = v[src] * attn[:, :, None]
            out = jax.ops.segment_sum(msg, dst, num_segments=n)
            return out.reshape(n, H * C) + bias
        src, dst = (edge_index[0], edge_index[1])
        return _forward(x, edge_weight, edge_attr, Wq, Wk, Wv, We, gate, bias, src, dst)

    def _L1_gnn_ref(h, src, dst, W1, b1, W2, b2):
        import jax, jax.numpy as jnp
        import numpy as np
        N, E, IN_DIM, HID, OUT = (50000, 9375, 128, 256, 128)
        n = h.shape[0]
        msg_sum = jax.ops.segment_sum(h[src], dst, num_segments=n)
        deg = jax.ops.segment_sum(jnp.ones((src.shape[0],), h.dtype), dst, num_segments=n)
        h_neigh = msg_sum / jnp.maximum(deg, 1.0)[:, None]
        h_total = jnp.concatenate([h, h_neigh], axis=1)
        out = (h_total @ W1 + b1) @ W2 + b2
        return jax.nn.relu(out)

    def _L2_gnn_ref(h, weight, src, dst, rel):
        import jax, jax.numpy as jnp
        import numpy as np
        N_NODES = 50000
        N_EDGES = 12500
        IN_FEAT = 128
        OUT_FEAT = 128
        NUM_REL = 8
        n_nodes = h.shape[0]
        hw = jnp.einsum('ni,rio->nro', h, weight)
        msg = hw[src, rel]
        out = jax.ops.segment_sum(msg, dst, num_segments=n_nodes)
        return out

    def _L3_gnn_ref(node_feature, W_e, b_e, W_n, b_n, edge_src, edge_dst, edge_type, node_type):
        import jax, jax.numpy as jnp
        import numpy as np
        N_NODES = 50000
        N_EDGES = 12500
        D = 128
        T = 3
        NODE_IN = D + T * D
        N, Din = node_feature.shape
        n_types = W_e.shape[0]
        out_dim = W_e.shape[1]
        src = node_feature[edge_src]
        parts = [jax.nn.relu(node_feature)]
        for t in range(n_types):
            msg = jax.nn.relu(src @ W_e[t].T + b_e[t])
            msg = jnp.where((edge_type == t)[:, None], msg, jnp.zeros((), msg.dtype))
            parts.append(jax.ops.segment_sum(msg, edge_dst, num_segments=N))
        agg = jnp.concatenate(parts, axis=1)
        updated = jnp.zeros((N, out_dim), node_feature.dtype)
        for t in range(n_types):
            o = agg @ W_n[t].T + b_n[t]
            updated = jnp.where((node_type == t)[:, None], o, updated)
        return updated + node_feature
    edge_index = jnp.stack([src, dst])
    x = _layernorm(x + _L0_gnn_ref(x, edge_index, edge_weight, edge_attr_64, L0_gnn_Wq, L0_gnn_Wk, L0_gnn_Wv, L0_gnn_We, L0_gnn_gate, L0_gnn_bias), axis=-1)
    x = _layernorm(x + _L1_gnn_ref(x, src, dst, L1_gnn_W1, L1_gnn_b1, L1_gnn_W2, L1_gnn_b2), axis=-1)
    x = _layernorm(x + _L2_gnn_ref(x, L2_gnn_weight, src, dst, edge_type_8), axis=-1)
    x = _layernorm(x + _L3_gnn_ref(x, L3_gnn_W_e, L3_gnn_b_e, L3_gnn_W_n, L3_gnn_b_n, src, dst, edge_type_3, node_type_3), axis=-1)
    return x

_drawn_inputs = setup_inputs


def setup_inputs(seed=0):
    import zlib

    import numpy as np

    out = dict(_drawn_inputs(seed))
    spreads = {'L0_gnn_gate': (1.0, 0.6),
     'L0_gnn_bias': (0.0, 0.1),
     'L3_gnn_b_e': (0.0, 0.8),
     'L3_gnn_b_n': (0.0, 0.1)}
    factors = {'edge_attr_64': 3.427,
     'edge_weight': 42.636,
     'L0_gnn_Wq': 64.0,
     'L0_gnn_Wk': 9.399,
     'L0_gnn_We': 3.296,
     'L1_gnn_b1': 3.616}
    for name, (base, spread) in spreads.items():
        noise = np.random.default_rng([zlib.crc32(name.encode()), seed]).standard_normal(out[name].shape)
        drawn = base * np.exp(spread * noise) if base else spread * noise
        out[name] = jnp.asarray(drawn.astype(out[name].dtype))
    for name, factor in factors.items():
        out[name] = (out[name] * factor).astype(out[name].dtype)
    return out
```

```python
from contextlib import ExitStack

import concourse.bass as bass
from concourse import mybir

F32 = mybir.dt.float32
BF16 = mybir.dt.bfloat16
I32 = mybir.dt.int32
ALU = mybir.AluOpType
ACT = mybir.ActivationFunctionType
AX_X = mybir.AxisListType.X

D = 128
R = 125
T = 4
C = R * T
EPS = 1e-5
TINY = 1e-16
BIG = 1e30
SKIP = 1 << 20
RSQRT_GUESS = 1597463007.0


class Lin:

    def __init__(self, a, s=0, it=None):
        self.a, self.s, self.it = a, s, it

    def __add__(self, n):
        return Lin(self.a + n, self.s, self.it)

    def __mul__(self, n):
        return Lin(self.a * n, self.s * n, self.it)

    def half(self):
        assert self.s % 2 == 0
        return Lin(self.a // 2, self.s // 2, self.it)

    def parity(self):
        return self.a % 2

    def v(self):
        return self.a if self.it is None or self.s == 0 else self.it * self.s + self.a


def at(count):
    if not isinstance(count, Lin):
        return max(count, 0)
    if count.it is None or count.s == 0:
        return max(count.a, 0)
    assert count.a > 0
    return count.v()


def settle(eng, sem):
    eng.sem_inc(sem, 1)


class Chain:

    def __init__(self, eng, sem):
        self.eng, self.sem, self.base, self.k, self.it, self.per = eng, sem, 0, 0, None, 0

    def step(self, ins):
        ins.then_inc(self.sem, 1)
        self.k += 1
        self.eng.wait_ge(self.sem, at(Lin(self.base + self.k, self.per, self.it)))

    def loop(self, it, per):
        self.base, self.k, self.it, self.per = self.base + self.k, 0, it, per

    def end(self, trips):
        assert self.k == self.per, f"{self.k} steps in the loop's body, {self.per} stated"
        self.base, self.k, self.it, self.per = self.base + trips * self.per, 0, None, 0


def gnn_kernel(nc, x, src, dst, eattrT, etype3, etype8, eweight, ntype3, Wq, Wk, Wv, We, gate,
               bias0, W1T, b1, W2, b2, Wr, WeT, beT, WnT, bn, ident_d, out):
    N, E = x.shape[0], src.shape[0]
    NC, EC = N // C, E // C
    PEEL = 3
    TR = (EC - PEEL) // 2
    H = gate.shape[0]
    HC = D // H
    ED = eattrT.shape[0]
    REL = Wr.shape[1]
    NT = WeT.shape[1]
    INV = float(HC) ** -0.5
    PM = E // R
    assert N % C == 0 and E % C == 0 and (EC - PEEL) % 2 == 0 and NC == 4 * EC

    rows = lambda a: a.rearrange("(n p j) d -> n p (j d)", p=R, j=T)
    x_c, out_c = rows(x), rows(out)
    src_c = src.rearrange("(n p j) -> n p j", p=R, j=T)
    dst_c = dst.rearrange("(n p j) -> n p j", p=R, j=T)
    nt_c = ntype3.rearrange("(n p j) o -> n p (j o)", p=R, j=T)

    s_rows = [nc.dram_tensor(f"source_rows{i}", [E, D], F32).ap() for i in (1, 2, 3)]
    d_rows = [nc.dram_tensor(f"target_rows{i}", [E, D], F32).ap() for i in (1, 2, 3)]
    same_d = nc.dram_tensor("same_d", [1, E], F32).ap()
    start_d = nc.dram_tensor("start_d", [1, E], F32).ap()
    last_d = nc.dram_tensor("last_d", [E], I32).ap()
    off_d = nc.dram_tensor("off_d", [NT, E], BF16).ap()
    slot_d = nc.dram_tensor("slot_d", [N, 1], I32).ap()
    last_c = last_d.rearrange("(n p j) -> n p j", p=R, j=T)

    ctx = ExitStack()
    with ctx:
        def sb(name, shape, dt=F32):
            return ctx.enter_context(nc.sbuf_tensor(name, shape, dt))

        def sem(name):
            return ctx.enter_context(nc.semaphore(name))

        def two(make, name, *a):
            return [make(f"{name}{i}", *a) for i in range(2)]

        wq, wk, wv = sb("wq", [D, D]), sb("wk", [D, D]), sb("wv", [D, D])
        qs, ks = sb("qs", [D, D]), sb("ks", [D, D])
        we, es = sb("we", [ED, D]), sb("es", [ED + 1, D])
        head = sb("head", [D, 3, H])
        gate_sb = sb("gate_sb", [ED + 1, H])
        w1t, w2 = sb("w1t", [D, 2, 2 * D]), sb("w2", [D, 2, D])
        b1c, b1m = sb("b1c", [D, 2]), sb("b1m", [D, 2, D])
        wab = sb("wab", [D, 2, D])
        wr, wet, wnt = sb("wr", [D, REL, D]), sb("wet", [D, NT, D]), sb("wnt", [D, 1 + NT, NT, D])
        bet = sb("bet", [D, NT])
        ident = sb("ident", [D, D])
        bias_bc = sb("bias_bc", [R, D])
        brow = sb("brow", [D, 2 + NT, D])
        b2row = sb("b2row", [D, D])
        brest = sb("brest", [D, 2 + NT, D])
        bhi, bmid, blo = (sb(n, [D, 2 + NT, D], BF16) for n in ("bhi", "bmid", "blo"))
        bparts = sb("bparts", [D, 2 + NT, T, D], BF16)
        ones_f = sb("ones_f", [D, 1])
        ones_bf = sb("ones_bf", [D, D], BF16)
        cur, prv, nxt = (sb(n, [R, PM], I32) for n in ("cur", "prv", "nxt"))
        ty = sb("ty", [R, PM], I32)
        same_p, start_p, more_p = (sb(n, [R, PM]) for n in ("same_p", "start_p", "more_p"))
        last_p = sb("last_p", [R, PM], I32)
        off_p = sb("off_p", [R, NT, PM], BF16)
        fill = sb("fill", [R, N // R], I32)
        eid = sb("eid", [R, EC, T], I32)
        slot_all, ntd_all = sb("slot_all", [R, EC, T], I32), sb("ntd_all", [R, EC, T], I32)
        xin, ntin = two(sb, "xin", [R, T, D]), two(sb, "ntin", [R, T], I32)
        y0, y1, sel = (sb(n, [R, T, D]) for n in ("y0", "y1", "sel"))
        x1, x3 = sb("x1", [R, T, D]), sb("x3", [R, T, D])
        xt = sb("xt", [D, T, R])
        rt = sb("rt", [D, T, R])
        res = two(sb, "res", [R, T, D])
        is_type = [two(sb, f"is_type{t}_", [R, T], I32) for t in range(1, NT)]
        bst = sb("bst", [R, 6 * T, 6])
        mv = sb("mv", [R, 6 * T, 2])
        ve, rst, nmr, tmp = (sb(n, [R, 6 * T]) for n in ("ve", "rst", "nmr", "tmp"))
        xs, xd = two(sb, "xs", [R, T, D]), two(sb, "xd", [R, T, D])
        isrc, idst, ilast, ieid = (two(sb, n, [R, T], I32) for n in ("isrc", "idst", "ilast", "ieid"))
        islot, intd = two(sb, "islot", [R, T], I32), two(sb, "intd", [R, T], I32)
        st, dt = sb("st", [D, R, T]), sb("dt", [D, R, T])
        stf, dtf = (a[:, :, :].rearrange("d p j -> d (p j)") for a in (st, dt))
        ea = two(sb, "ea", [ED + 1, C])
        same = two(sb, "same", [D, C])
        aux = two(sb, "aux", [D, C])
        rel = two(sb, "rel", [D, C], I32)
        off = two(sb, "off", [1, NT, C], BF16)
        run = sb("run", [D, 3, C + 1])
        wa, wb, wc = sb("wa", [D, C]), sb("wb", [D, C]), sb("wc", [D, C])
        agg = sb("agg", [D, R, T])
        aggf = agg[:, :, :].rearrange("d p j -> d (p j)")
        ys, yd = sb("ys", [R, T, D]), sb("yd", [R, T, D])
        so, so3, do = (two(sb, n, [R, T, D]) for n in ("so", "so3", "do"))
        sel_e = ys

        bank = [ctx.enter_context(nc.psum_tensor(f"bank{i}", [D, 512], F32)) for i in range(8)]
        pt, pz, po = bank[0], bank[1], bank[2:5]
        pa, pb, pc = bank[5:8]

        s_w, s_idx, s_slotrow, s_prep, s_scr, s_pe0, s_bp, s_const = map(
            sem, ("s_w", "s_idx", "s_slotrow", "s_prep", "s_scr", "s_pe0", "s_bp", "s_const"))
        s_fill, s_passed = sem("s_fill"), sem("s_passed")
        s_xin, s_res = two(sem, "s_xin"), two(sem, "s_res")
        s_y0, s_ln, s_x1, s_x3, s_out = map(sem, ("s_y0", "s_ln", "s_x1", "s_x3", "s_out"))
        s_tx, s_xt, s_z, s_tr, s_rt, s_o, s_sel = map(sem, ("s_tx", "s_xt", "s_z", "s_tr", "s_rt", "s_o", "s_sel"))
        s_chain, s_pchain, s_achain = sem("s_chain"), sem("s_pchain"), sem("s_achain")

        SINGLE = ("tS tD eS eD pA pB pR vA vE eX vN nS nD", "tS tD eS eD pR vA vN nS nD",
                  "tS eS pM pR vA vM vN nD", "tS tD eS eD pM pR vA eX vN nD sel")
        PAIRS = ("aux idx g stS stD sc", "ld aux g gi stS stD", "ld aux g gi stD", "ld aux g sc")

        ph = [{**{k: sem(f"layer{n}_{k}") for k in SINGLE[n].split()},
               **{k: two(sem, f"layer{n}_{k}_") for k in PAIRS[n].split()}} for n in range(4)]

        def counted(chunk, per):
            return (chunk.half() + 1) * per

        def over(eng, body, chain=None, per=0):
            for c in range(PEEL):
                body(Lin(c))
            with eng.Fori(0, TR) as it:
                if chain:
                    chain.loop(it, per)
                body(Lin(PEEL, 2, it))
                body(Lin(PEEL + 1, 2, it))
            if chain:
                chain.end(TR)

        def dense_of(p, c):
            if p == 0:
                return [c * 2, c * 2 + 1]
            return [c + (2 * EC if p == 1 else 3 * EC)] if p < 3 else []

        NLOADS = 16 + NT
        DVE_STEPS = (108, 66, 60, 34)
        one_row = ones_f[:, 0:1].broadcast_to([D, C])
        run_tile = lambda k, j: run[:, k, 1:C + 1].rearrange("d (p j) -> d p j", j=T)[:, :, j]
        block = ctx.enter_context(nc.Block())

        @block.sync
        def _(sp):
            pm = lambda a: a.rearrange("(p t) -> p t", t=PM)
            sp.wait_ge(s_const, 1)
            sp.dma_start(cur[:, :], pm(dst)).then_inc(s_idx, 16)
            sp.dma_start(prv[1:R, :], bass.AP(dst.tensor, PM - 1, [[PM, R - 1], [1, PM]])).then_inc(s_idx, 16)
            sp.dma_start(prv[0:1, 1:PM], bass.AP(dst.tensor, 0, [[PM, 1], [1, PM - 1]])).then_inc(s_idx, 16)
            sp.dma_start(nxt[0:R - 1, :], bass.AP(dst.tensor, 1, [[PM, R - 1], [1, PM]])).then_inc(s_idx, 16)
            sp.dma_start(nxt[R - 1:R, 0:PM - 1], bass.AP(dst.tensor, E - PM + 1, [[PM, 1], [1, PM - 1]])).then_inc(s_idx, 16)
            sp.dma_start(ty[:, :], pm(etype3)).then_inc(s_idx, 16)
            loads = [(ident[:, :], ident_d), (bias_bc[:, :], bias0[0:1, :].broadcast_to([R, D])),
                     (wq[:, :], Wq), (wk[:, :], Wk), (wv[:, :], Wv), (we[:, :], We),
                     (gate_sb[ED:ED + 1, :], gate[None, :]), (w1t[:, :, :], W1T), (w2[:, :, :], W2),
                     (b1c[:, :], b1), (b2row[:, :], b2[0:1, :].broadcast_to([D, D])),
                     (brow[:, 1, :], bias0[0:1, :].broadcast_to([D, D])),
                     (wr[:, :, :], Wr), (wet[:, :, :], WeT), (wnt[:, :, :, :], WnT), (bet[:, :], beT)]
            loads += [(brow[:, 2 + t, :], bn[t:t + 1, :].broadcast_to([D, D])) for t in range(NT)]
            for to, of in loads:
                sp.dma_start(to, of).then_inc(s_w, 16)
            sp.wait_ge(s_prep, 1)
            sp.wait_ge(s_fill, 1)
            row = lambda a: a.rearrange("o (p t) -> (o p) t", t=PM)
            sp.dma_start(slot_d.rearrange("(p t) o -> p (t o)", p=R), fill[:, :]).then_inc(s_slotrow, 16)
            sp.dma_start(row(same_d), same_p[:, :]).then_inc(s_scr, 16)
            sp.dma_start(row(start_d), start_p[:, :]).then_inc(s_scr, 16)
            sp.dma_start(pm(last_d), last_p[:, :]).then_inc(s_scr, 16)
            for t in range(NT):
                sp.dma_start(off_d[t].rearrange("(p t) -> p t", t=PM), off_p[:, t, :]).then_inc(s_scr, 16)
            sp.wait_ge(s_scr, 16 * (3 + NT))

            def load_dense(d):
                b = d.parity()
                sp.wait_ge(s_ln, at(d + (-1)))
                sp.dma_start(xin[b][:, :, :].rearrange("p j d -> p (j d)"), x_c[d.v()]).then_inc(s_xin[b], 16)
                sp.dma_start(ntin[b][:, :], nt_c[d.v()]).then_inc(s_xin[b], 16)

            def store_dense(d):
                b = d.parity()
                sp.wait_ge(s_out, at(d + 1))
                sp.dma_start(out_c[d.v()], res[b][:, :, :].rearrange("p j d -> p (j d)")).then_inc(s_res[b], 16)

            def load_edges(p, c):
                b, q = c.parity(), ph[p]
                cols = bass.ds(c.v() * C, C)
                sp.wait_ge(q["nD"], at(c + (-1)))
                if p == 0:
                    sp.wait_ge(q["g"][b], at(c.half() * (32 * T)))
                    sp.wait_ge(q["sc"][b], at(c.half() * (16 * T)))
                    sp.dma_start(isrc[b][:, :], src_c[c.v()]).then_inc(q["idx"][b], 16)
                    sp.dma_start(idst[b][:, :], dst_c[c.v()]).then_inc(q["idx"][b], 16)
                    sp.dma_start(ilast[b][:, :], last_c[c.v()]).then_inc(q["idx"][b], 16)
                    sp.dma_start(ea[b][0:ED, :], eattrT[:, cols]).then_inc(q["aux"][b], 16)
                    sp.dma_start(ea[b][ED:ED + 1, :], eweight[0:1, cols]).then_inc(q["aux"][b], 16)
                    sp.dma_start(same[b][:, :], same_d[0:1, cols].broadcast_to([D, C])).then_inc(q["aux"][b], 16)
                    sp.dma_start(aux[b][:, :], start_d[0:1, cols].broadcast_to([D, C])).then_inc(q["aux"][b], 16)
                    return
                flat = lambda a: a[:, :, :].rearrange("p j d -> p (j d)")
                sp.dma_start(flat(xs[b]), rows(s_rows[p - 1])[c.v()]).then_inc(q["ld"][b], 16)
                sp.dma_start(flat(xd[b]), rows(d_rows[p - 1])[c.v()]).then_inc(q["aux"][b], 16)
                sp.dma_start(same[b][:, :], same_d[0:1, cols].broadcast_to([D, C])).then_inc(q["aux"][b], 16)
                if p == 1:
                    sp.dma_start(isrc[b][:, :], src_c[c.v()]).then_inc(q["ld"][b], 16)
                if p == 2:
                    sp.dma_start(idst[b][:, :], dst_c[c.v()]).then_inc(q["ld"][b], 16)
                    sp.dma_start(rel[b][:, :], etype8[0:1, cols].broadcast_to([D, C])).then_inc(q["aux"][b], 16)
                if p == 3:
                    sp.wait_ge(q["sc"][b], at(c.half() * (16 * T)))
                    sp.dma_start(ilast[b][:, :], last_c[c.v()]).then_inc(q["ld"][b], 16)
                    sp.dma_start(off[b][:, :, :], off_d[:, cols][None]).then_inc(q["aux"][b], 16)

            def store_edges(p, c):
                b, q = c.parity(), ph[p]
                flat = lambda a: a[:, :, :].rearrange("p j d -> p (j d)")
                if p < 2:
                    sp.wait_ge(q["nS"], at(c + 1))
                    sp.dma_start(rows(s_rows[p])[c.v()], flat(so[b])).then_inc(q["stS"][b], 16)
                if p == 1:
                    sp.dma_start(rows(s_rows[2])[c.v()], flat(so3[b])).then_inc(q["stS"][b], 16)
                sp.wait_ge(q["nD"], at(c + 1))
                sp.dma_start(rows(d_rows[p])[c.v()], flat(do[b])).then_inc(q["stD"][b], 16)

            for p in range(4):
                if p == 0:
                    load_edges(0, Lin(0))
                    load_dense(Lin(0))

                def body(c, last=False):
                    if not last:
                        load_edges(p, c + 1)
                    for d in dense_of(p, c):
                        if not (last and p == 2):
                            load_dense(d + 1)
                        if d.it is not None or d.a >= 2:
                            store_dense(d + (-2))
                    if p < 3:
                        store_edges(p, c)

                if p > 0:
                    q = ph[p - 1]
                    for b in range(2):
                        n = (EC + 1 - b) // 2
                        if p < 3:
                            sp.wait_ge(q["stS"][b], at(16 * n * (2 if p == 2 else 1)))
                        sp.wait_ge(q["stD"][b], at(16 * n))
                    load_edges(p, Lin(0))
                for c in range(PEEL):
                    body(Lin(c))
                with sp.Fori(0, TR - 1) as it:
                    body(Lin(PEEL, 2, it))
                    body(Lin(PEEL + 1, 2, it))
                body(Lin(EC - 2))
                body(Lin(EC - 1), last=True)
                if p == 2:
                    for d in range(NC - 2, NC):
                        store_dense(Lin(d))

        bc = lambda a: a.unsqueeze(2).broadcast_to([R, T, D])
        tile_of = lambda a, j: a[:, j * R:(j + 1) * R]
        flat_bank = lambda k: k[0:R, 0:T * D].rearrange("p (j d) -> p j d", j=T)
        by_tile = lambda k: k[:, 0:C].rearrange("d (j p) -> d j p", j=T)

        @block.gpsimd
        def _(pool):
            chain = Chain(pool, s_pchain)
            nc.gpsimd.memset(prv[:, :], -1)
            nc.gpsimd.memset(nxt[:, :], -1).then_inc(s_const, 1)
            nc.gpsimd.memset(fill[:, :], SKIP).then_inc(s_fill, 1)
            nc.gpsimd.iota(eid[:, :, :], pattern=[[C, EC], [1, T]], base=0, channel_multiplier=T)
            nc.gpsimd.memset(ones_f[:, :], 1.0)
            chain.step(nc.gpsimd.memset(ones_bf[:, :], 1.0))

            def gather(to, table, index, j, bound):
                if j == 0:
                    settle(pool, s_passed)
                return nc.gpsimd.indirect_dma_start(
                    out=to, out_offset=None, in_=table,
                    in_offset=bass.IndirectOffsetOnAxis(ap=index[:, j:j + 1], axis=0),
                    bounds_check=bound, oob_is_err=False)

            def scatter(table, index, j, of):
                if j == 0:
                    settle(pool, s_passed)
                return nc.gpsimd.indirect_dma_start(
                    out=table, out_offset=bass.IndirectOffsetOnAxis(ap=index[:, j:j + 1], axis=0),
                    in_=of, in_offset=None, bounds_check=N - 1, oob_is_err=False)

            def layer0(c):
                b, q = c.parity(), ph[0]
                pool.wait_ge(q["idx"][b], at(counted(c, 48)))
                pool.wait_ge(q["nD"], at(c + (-1)))
                for j in range(T):
                    gather(xs[b][:, j, :], x, isrc[b], j, N - 1).then_inc(q["g"][b], 16)
                    gather(xd[b][:, j, :], x, idst[b], j, N - 1).then_inc(q["g"][b], 16)
                chain.step(nc.gpsimd.tensor_copy(ieid[b][:, :], eid[:, c.v(), :]))
                if c.it is None and c.a == 0:
                    pool.wait_ge(s_slotrow, 16)
                for j in range(T):
                    scatter(slot_d, ilast[b], j, ieid[b][:, j:j + 1]).then_inc(q["sc"][b], 16)

            def layer1(c):
                b, q = c.parity(), ph[1]
                pool.wait_ge(q["ld"][b], at(counted(c, 32)))
                for j in range(T):
                    gather(islot[b][:, j:j + 1], slot_d, isrc[b], j, N - 1).then_inc(q["gi"][b], 16)
                pool.wait_ge(q["gi"][b], at(counted(c, 16 * T)))
                for j in range(T):
                    gather(xs[b][:, j, :], d_rows[0], islot[b], j, E - 1).then_inc(q["g"][b], 16)
                chain.step(nc.gpsimd.tensor_copy(slot_all[:, c.v(), :], islot[b][:, :]))
                settle(pool, s_passed)

            def layer2(c):
                b, q = c.parity(), ph[2]
                pool.wait_ge(q["g"][b], at(c.half() * (16 * T)))
                settle(pool, s_passed)
                chain.step(nc.gpsimd.tensor_copy(islot[b][:, :], slot_all[:, c.v(), :]))
                pool.wait_ge(q["ld"][b], at(counted(c, 32)))
                for j in range(T):
                    gather(intd[b][:, j:j + 1], ntype3, idst[b], j, N - 1).then_inc(q["gi"][b], 16)
                for j in range(T):
                    gather(xs[b][:, j, :], d_rows[1], islot[b], j, E - 1).then_inc(q["g"][b], 16)
                pool.wait_ge(q["gi"][b], at(counted(c, 16 * T)))
                settle(pool, s_passed)
                chain.step(nc.gpsimd.tensor_copy(ntd_all[:, c.v(), :], intd[b][:, :]))
                settle(pool, s_passed)

            def store(c):
                b, q = c.parity(), ph[3]
                pool.wait_ge(q["nD"], at(c + 1))
                for j in range(T):
                    scatter(out, ilast[b], j, do[b][:, j, :]).then_inc(q["sc"][b], 16)

            def layer3(c):
                b, q = c.parity(), ph[3]
                pool.wait_ge(q["g"][b], at(c.half() * (16 * T)))
                settle(pool, s_passed)
                chain.step(nc.gpsimd.tensor_copy(islot[b][:, :], slot_all[:, c.v(), :]))
                pool.wait_ge(q["ld"][b], at(counted(c, 32)))
                for j in range(T):
                    gather(xs[b][:, j, :], d_rows[2], islot[b], j, E - 1).then_inc(q["g"][b], 16)
                if c.it is None and c.a == 0:
                    for k in range(2):
                        pool.wait_ge(s_res[k], 16 * (NC // 2))
                else:
                    store(c + (-1))

            def landed(p):
                for b in range(2):
                    n = (EC + 1 - b) // 2
                    if p == 1:
                        pool.wait_ge(ph[0]["sc"][b], 16 * T * n)
                    if p > 0:
                        pool.wait_ge(ph[p - 1]["stD"][b], 16 * n)
                        pool.wait_ge(ph[p - 1]["g"][b], (32 if p == 1 else 16) * T * n)

            for p, layer, steps in ((0, layer0, 1), (1, layer1, 1), (2, layer2, 2), (3, layer3, 1)):
                landed(p)
                over(pool, layer, chain, 2 * steps)
            store(Lin(EC - 1))
            for b in range(2):
                pool.wait_ge(ph[3]["sc"][b], 16 * T * ((EC + 1 - b) // 2))

        @block.vector
        def _(dve):
            V = nc.vector
            chain = Chain(dve, s_chain)
            step = chain.step
            dve.wait_ge(s_idx, 96)
            V.tensor_tensor(same_p[:, :], cur[:, :], prv[:, :], ALU.is_equal)
            V.tensor_tensor(more_p[:, :], cur[:, :], nxt[:, :], ALU.is_equal)
            for t in range(NT):
                V.tensor_scalar(off_p[:, t, :], ty[:, :], t, -BIG, ALU.not_equal, ALU.mult)
            step(V.memset(run[:, :, :], 0.0))
            V.tensor_scalar(start_p[:, :], same_p[:, :], -1.0, BIG, ALU.add, ALU.mult)
            V.scalar_tensor_tensor(out=last_p[:, :], in0=more_p[:, :], scalar=float(SKIP), in1=cur[:, :],
                                   op0=ALU.mult, op1=ALU.add).then_inc(s_prep, 1)
            dve.wait_ge(s_w, 16 * NLOADS)
            for i, w in enumerate((wq, wk)):
                V.tensor_reduce(head[:, i, :], w[:, :].rearrange("k (h c) -> k h c", h=H), AX_X, ALU.add)
            V.tensor_reduce(head[0:ED, 2, :], we[:, :].rearrange("k (h c) -> k h c", h=H), AX_X, ALU.add)
            V.tensor_copy(b1m[:, :, :], b1c[:, :].unsqueeze(2).broadcast_to([D, 2, D]))
            step(V.memset(bparts[:, :, :, :], 0.0))
            heads = lambda a, n: a.unsqueeze(2).broadcast_to([n, H, HC])
            for i, w in enumerate((qs, ks)):
                V.tensor_scalar(w[:, :].rearrange("k (h c) -> k h c", h=H), heads(head[:, i, :], D), INV, None, ALU.mult)
            V.tensor_scalar(es[0:ED, :].rearrange("k (h c) -> k h c", h=H), heads(head[0:ED, 2, :], ED), INV, None, ALU.mult)
            V.tensor_copy(es[ED:ED + 1, :].rearrange("k (h c) -> k h c", h=H),
                          heads(gate_sb[ED:ED + 1, :], 1)).then_inc(s_bp, 1)
            dve.wait_ge(s_pe0, 1)
            V.tensor_copy(wab[:, :, :], bank[1][:, 0:2 * D].rearrange("k (a d) -> k a d", a=2))
            step(V.tensor_tensor(brow[:, 0, :], bank[0][:, 0:D], b2row[:, :], ALU.add))
            step(V.tensor_copy(bhi[:, :, :], brow[:, :, :]))
            step(V.tensor_tensor(brest[:, :, :], brow[:, :, :], bhi[:, :, :], ALU.subtract))
            step(V.tensor_copy(bmid[:, :, :], brest[:, :, :]))
            step(V.tensor_tensor(brest[:, :, :], brest[:, :, :], bmid[:, :, :], ALU.subtract))
            step(V.tensor_copy(blo[:, :, :], brest[:, :, :]))
            for part, p in ((bhi, 0), (bmid, 32), (blo, 64)):
                for j in range(T):
                    last = V.tensor_copy(bparts[p:p + 1, :, j, :], part[p:p + 1, :, :])
            last.then_inc(s_bp, 1)

            def aggregate(groups):
                settle(dve, s_passed)
                for g in groups:
                    for j in range(T):
                        last = V.bn_aggr(mv[:, g * T + j, :], bst[:, g * T + j, :])
                step(last)

            def stats(y, g):
                for j in range(T):
                    last = V.bn_stats(bst[:, g * T + j, :], y[:, j, :])
                return last

            def rsqrt(lo, hi, twice, done):
                g = slice(lo * T, hi * T)
                for k in range(lo, hi):
                    a = slice(k * T, (k + 1) * T)
                    if k in twice:
                        last = V.tensor_scalar(ve[:, a], mv[:, a, 1], 1.0 + EPS, EPS * EPS, ALU.mult, ALU.add)
                    else:
                        last = V.tensor_scalar(ve[:, a], mv[:, a, 1], EPS, None, ALU.add)
                step(last)
                step(V.tensor_scalar(rst[:, g].bitcast(I32), ve[:, g].bitcast(I32), -0.5, RSQRT_GUESS, ALU.mult, ALU.add))
                for _ in range(3):
                    step(V.scalar_tensor_tensor(out=tmp[:, g], in0=rst[:, g], scalar=-0.5, in1=rst[:, g], op0=ALU.mult, op1=ALU.mult))
                    step(V.tensor_tensor(tmp[:, g], tmp[:, g], ve[:, g], ALU.mult))
                    step(V.scalar_tensor_tensor(out=rst[:, g], in0=tmp[:, g], scalar=1.5, in1=rst[:, g], op0=ALU.add, op1=ALU.mult))
                V.scalar_tensor_tensor(out=nmr[:, g], in0=mv[:, g, 0], scalar=-1.0, in1=rst[:, g],
                                       op0=ALU.mult, op1=ALU.mult).then_inc(done, 1)

            def dense(d, extra=None):
                fixed = d.it is None
                first, second, third = (not fixed or 0 <= d.a - k < NC for k in range(3))
                dve.wait_ge(s_x1, at(d if not fixed else min(d.a, NC)))
                if fixed and d.a > NC:
                    dve.wait_ge(s_out, at(d.a - 2))
                    dve.wait_ge(s_x3, at(d.a - 1))
                b = d.parity()
                if third:
                    dve.wait_ge(s_sel, at(d + (-1)))
                    settle(dve, s_passed)
                    step(V.copy_predicated(sel[:, :, :], bc(is_type[0][b][:, :]), flat_bank(po[1])))
                if second:
                    dve.wait_ge(s_z, at(d))
                    V.scalar_tensor_tensor(out=y1[:, :, :], in0=flat_bank(pz), scalar=0.0, in1=x1[:, :, :],
                                           op0=ALU.max, op1=ALU.add)
                if third:
                    settle(dve, s_passed)
                    step(V.copy_predicated(sel[:, :, :], bc(is_type[1][b][:, :]), flat_bank(po[2])))
                if first:
                    dve.wait_ge(s_xin[b], at(counted(d, 32)))
                    for t in range(1, NT):
                        V.tensor_scalar(is_type[t - 1][b][:, :], ntin[b][:, :], t, None, ALU.is_equal)
                    V.tensor_tensor(y0[:, :, :], xin[b][:, :, :], bias_bc[:, :].unsqueeze(1).broadcast_to([R, T, D]), ALU.add)
                if third:
                    V.scalar_tensor_tensor(out=sel[:, :, :], in0=x3[:, :, :], scalar=2.0, in1=sel[:, :, :],
                                           op0=ALU.mult, op1=ALU.add)
                if extra:
                    extra()
                step(V.memset(tmp[0:1, 0:1], 0.0))
                if second:
                    stats(y1, 1)
                if first:
                    stats(y0, 2)
                if extra:
                    stats(ys, 3)
                if third:
                    stats(sel, 0)
                step(V.memset(tmp[0:1, 0:1], 0.0))
                lo, hi = (0 if third else 1 if second else 2), (4 if extra else 3 if first else 2 if second else 1)
                aggregate(range(lo, hi))
                rsqrt(lo, hi, (1,), s_ln)

            carry = lambda n: V.tensor_copy(run[:, 0:n, 0:1], run[:, 0:n, C:C + 1])

            def scan(k, data0, data1, op0, op1):
                return V.tensor_tensor_scan(run[:, k, 1:C + 1], data0, data1, run[:, k, 0:1], op0, op1)

            def target_rows(c, q, source, relu):
                b = c.parity()
                dve.wait_ge(q["nD"], at(c))
                if relu:
                    V.scalar_tensor_tensor(out=yd[:, :, :], in0=flat_bank(source), scalar=0.0, in1=xd[b][:, :, :],
                                           op0=ALU.max, op1=ALU.add)
                else:
                    step(V.tensor_tensor(yd[:, :, :], xd[b][:, :, :], flat_bank(source), ALU.add))

            def layer0(c):
                b, q = c.parity(), ph[0]
                d0, d1 = dense_of(0, c)

                def source_rows():
                    dve.wait_ge(q["g"][b], at(counted(c, 32 * T)))
                    dve.wait_ge(q["nS"], at(c))
                    V.tensor_tensor(ys[:, :, :], xs[b][:, :, :], bias_bc[:, :].unsqueeze(1).broadcast_to([R, T, D]), ALU.add)

                dense(d0, source_rows)
                dve.wait_ge(q["pA"], at(c + 1))
                dve.wait_ge(q["aux"][b], at(counted(c, 64)))
                dve.wait_ge(q["pR"], at(c))
                step(V.tensor_scalar(wc[:, :], pc[:, 0:C], 0.2, None, ALU.mult))
                step(V.tensor_tensor(wa[:, :], wc[:, :], pc[:, 0:C], ALU.max))
                step(scan(0, aux[b][:, :], wa[:, :], ALU.add, ALU.max))
                step(V.tensor_tensor(wb[:, :], run[:, 0, 0:C], aux[b][:, :], ALU.add))
                V.tensor_tensor(wa[:, :], wa[:, :], run[:, 0, 1:C + 1], ALU.subtract)
                V.tensor_tensor(wb[:, :], wb[:, :], run[:, 0, 1:C + 1], ALU.subtract).then_inc(q["vE"], 1)
                dense(d1)
                dve.wait_ge(q["eX"], at(c + 1))
                dve.wait_ge(q["pB"], at(c + 1))
                scan(2, wb[:, :], wa[:, :], ALU.mult, ALU.add)
                step(V.tensor_tensor(wc[:, :], pa[:, 0:C], wa[:, :], ALU.mult))
                step(scan(1, wb[:, :], wc[:, :], ALU.mult, ALU.add))
                carry(3)
                step(V.tensor_scalar(wc[:, :], run[:, 2, 1:C + 1], TINY, None, ALU.add))
                step(V.reciprocal(wc[:, :], wc[:, :]))
                V.tensor_tensor(aggf, run[:, 1, 1:C + 1], wc[:, :], ALU.mult).then_inc(q["vA"], 1)
                dve.wait_ge(q["pR"], at(c + 1))
                target_rows(c, q, pb, False)
                step(stats(yd, 5))
                aggregate((5,))
                rsqrt(5, 6, (), q["vN"])

            def layer1(c):
                b, q = c.parity(), ph[1]
                dve.wait_ge(q["eS"], at(c + 1))
                dve.wait_ge(q["aux"][b], at(counted(c, 32)))
                dve.wait_ge(q["pR"], at(c))
                scan(0, same[b][:, :], stf, ALU.mult, ALU.add)
                step(scan(1, same[b][:, :], one_row, ALU.mult, ALU.add))
                carry(2)
                step(V.reciprocal(wc[:, :], run[:, 1, 1:C + 1]))
                V.tensor_tensor(aggf, run[:, 0, 1:C + 1], wc[:, :], ALU.mult).then_inc(q["vA"], 1)
                dense(dense_of(1, c)[0])
                dve.wait_ge(q["pR"], at(c + 1))
                dve.wait_ge(q["nS"], at(c))
                V.scalar_tensor_tensor(out=ys[:, :, :], in0=flat_bank(pa), scalar=0.0, in1=xs[b][:, :, :],
                                       op0=ALU.max, op1=ALU.add)
                target_rows(c, q, pb, True)
                step(V.memset(tmp[0:1, 0:1], 0.0))
                stats(ys, 3)
                step(stats(yd, 5))
                aggregate((3, 5))
                step(V.tensor_copy(mv[:, 4 * T:5 * T, :], mv[:, 3 * T:4 * T, :]))
                rsqrt(3, 6, (4,), q["vN"])

            def layer2(c):
                b, q = c.parity(), ph[2]
                dve.wait_ge(q["eS"], at(c + 1))
                dve.wait_ge(q["aux"][b], at(counted(c, 48)))
                for r in range(REL):
                    if r >= 2:
                        dve.wait_ge(q["pM"], at(c * REL + (r - 1)))
                    V.scalar_tensor_tensor(out=(wa, wb)[r % 2][:, :], in0=rel[b][:, :], scalar=float(r), in1=stf,
                                           op0=ALU.is_equal, op1=ALU.mult).then_inc(q["vM"], 1)
                dense(dense_of(2, c)[0])
                dve.wait_ge(q["pM"], at((c + 1) * REL))
                dve.wait_ge(q["pR"], at(c))
                scan(0, same[b][:, :], pb[:, 0:C], ALU.mult, ALU.add).then_inc(q["vA"], 1)
                dve.wait_ge(q["vA"], at(c + 1))
                carry(1)
                dve.wait_ge(q["pR"], at(c + 1))
                target_rows(c, q, pa, False)
                step(stats(yd, 5))
                aggregate((5,))
                rsqrt(5, 6, (), q["vN"])

            def layer3(c):
                b, q = c.parity(), ph[3]
                dve.wait_ge(q["aux"][b], at(counted(c, 48)))
                dve.wait_ge(q["pR"], at(c))
                for t, m in enumerate((wa, wb, wc)):
                    dve.wait_ge(q["eX"], at(c * NT + (t + 1)))
                    scan(t, same[b][:, :], m[:, :], ALU.mult, ALU.add).then_inc(q["vA"], 1)
                for t in range(1, NT):
                    last = V.tensor_scalar(is_type[t - 1][0][:, :], ntd_all[:, c.v(), :], t, None, ALU.is_equal)
                step(last)
                dve.wait_ge(q["vA"], at((c + 1) * NT))
                carry(NT)
                dve.wait_ge(q["sel"], at(c + 1))
                settle(dve, s_passed)
                step(V.copy_predicated(ys[:, :, :], bc(is_type[0][0][:, :]), flat_bank(bank[6])))
                settle(dve, s_passed)
                step(V.copy_predicated(ys[:, :, :], bc(is_type[1][0][:, :]), flat_bank(bank[7])))
                dve.wait_ge(q["nD"], at(c))
                step(V.scalar_tensor_tensor(out=yd[:, :, :], in0=xd[b][:, :, :], scalar=2.0, in1=ys[:, :, :],
                                            op0=ALU.mult, op1=ALU.add))
                step(stats(yd, 5))
                aggregate((5,))
                rsqrt(5, 6, (), q["vN"])

            for p, (layer, per) in enumerate(((layer0, DVE_STEPS[0]), (layer1, DVE_STEPS[1]),
                                              (layer2, DVE_STEPS[2]), (layer3, DVE_STEPS[3]))):
                if p:
                    step(V.memset(run[:, :, 0:1], 0.0))
                over(dve, layer, chain, per)
                if p == 2:
                    dense(Lin(NC))
                    dense(Lin(NC + 1))

        @block.scalar
        def _(act):
            A = nc.scalar.activation

            def normalize(to, y, g):
                for j in range(T):
                    k = g * T + j
                    last = A(to[:, j, :], y[:, j, :], ACT.Identity, scale=rst[:, k:k + 1], bias=nmr[:, k:k + 1])
                return last

            def dense(d, extra=None):
                fixed = d.it is None
                first, second, third = (not fixed or 0 <= d.a - k < NC for k in range(3))
                b = d.parity()
                act.wait_ge(s_ln, at(d + 1))
                if third:
                    act.wait_ge(s_res[b], at((d + (-2)).half() * 16))
                    normalize(res[b], sel, 0).then_inc(s_out, 1)
                if second:
                    normalize(x3, y1, 1).then_inc(s_x3, 1)
                if extra:
                    extra()
                if first:
                    normalize(x1, y0, 2).then_inc(s_x1, 1)
                if second:
                    act.wait_ge(s_tr, at(d))
                    A(rt[:, :, :], by_tile(pt), ACT.Relu).then_inc(s_rt, 1)
                if first:
                    act.wait_ge(s_tx, at(d + 1))
                    A(xt[:, :, :], by_tile(pt), ACT.Copy).then_inc(s_xt, 1)
                if second:
                    act.wait_ge(s_o, at(d))
                    if third:
                        act.wait_ge(s_out, at(d + (-1)))
                    A(sel[:, :, :], flat_bank(po[0]), ACT.Copy).then_inc(s_sel, 1)

            natural = lambda a: a[:, :, :].rearrange("d p j -> d j p")

            def transposed(c, q, target=True, k=(5, 6), relu=False):
                act.wait_ge(q["tS"], at(c + 1))
                A(natural(st), by_tile(bank[k[0]]), ACT.Copy).then_inc(q["eS"], 1)
                if target:
                    act.wait_ge(q["tD"], at(c + 1))
                    A(natural(dt), by_tile(bank[k[1]]), ACT.Relu if relu else ACT.Copy).then_inc(q["eD"], 1)

            def target_rows(c, p):
                b, q = c.parity(), ph[p]
                act.wait_ge(q["vN"], at(c + 1))
                if p < 3:
                    act.wait_ge(q["stD"][b], at(c.half() * 16))
                else:
                    act.wait_ge(q["sc"][b], at(c.half() * (16 * T)))
                normalize(do[b], yd, 5).then_inc(q["nD"], 1)

            def layer0(c):
                b, q = c.parity(), ph[0]
                d0, d1 = dense_of(0, c)
                transposed(c, q)

                def source_rows():
                    act.wait_ge(q["stS"][b], at(c.half() * 16))
                    normalize(so[b], ys, 3).then_inc(q["nS"], 1)

                dense(d0, source_rows)
                act.wait_ge(q["vE"], at(c + 1))
                A(wb[:, :], wb[:, :], ACT.Exp)
                A(wa[:, :], wa[:, :], ACT.Exp).then_inc(q["eX"], 1)
                dense(d1)
                target_rows(c, 0)

            def layer1(c):
                b, q = c.parity(), ph[1]
                transposed(c, q)
                dense(dense_of(1, c)[0])
                act.wait_ge(q["vN"], at(c + 1))
                act.wait_ge(q["stS"][b], at(c.half() * 32))
                normalize(so[b], ys, 3)
                normalize(so3[b], ys, 4).then_inc(q["nS"], 1)
                target_rows(c, 1)

            def layer2(c):
                transposed(c, ph[2], target=False)
                dense(dense_of(2, c)[0])
                target_rows(c, 2)

            def layer3(c):
                q = ph[3]
                transposed(c, q, k=(0, 1), relu=True)
                for t, m in enumerate((wa, wb, wc)):
                    act.wait_ge(q["pM"], at(c * NT + (t + 1)))
                    act.wait_ge(q["vA"], at(c * NT))
                    A(m[:, :], bank[2 + t][:, 0:C], ACT.Relu, bias=bet[:, t:t + 1]).then_inc(q["eX"], 1)
                act.wait_ge(q["pR"], at(c + 1))
                act.wait_ge(q["nD"], at(c))
                A(ys[:, :, :], flat_bank(bank[5]), ACT.Copy).then_inc(q["sel"], 1)
                target_rows(c, 3)

            act.wait_ge(s_w, 16 * NLOADS)
            for p, layer in enumerate((layer0, layer1, layer2, layer3)):
                over(act, layer)
                if p == 2:
                    dense(Lin(NC))
                    dense(Lin(NC + 1))

        @block.tensor
        def _(pe):
            mm = nc.tensor.matmul

            def turn(to, rows_):
                for j in range(T):
                    last = nc.tensor.transpose(tile_of(to, j), rows_[:, j, :], ident[0:R, 0:R])
                return last

            def biased(to, i):
                mm(to[0:R, 0:T * D], ones_bf[:, 0:R], bparts[:, i, :, :].rearrange("k j d -> k (j d)"), start=True, stop=False, skip_group_check=True)

            def product(to, left, right, stop=True):
                for j in range(T):
                    last = mm(to[0:R, j * D:(j + 1) * D], left(j), right, start=False, stop=stop and j == T - 1, skip_group_check=True)
                return last

            pe.wait_ge(s_w, 16 * NLOADS)
            pe.wait_ge(s_bp, 1)
            for k in range(2):
                mm(bank[0][:, 0:D], b1m[:, k, :], w2[:, k, :], start=k == 0, stop=k == 1)
            for a in range(2):
                for k in range(2):
                    last = mm(bank[1][:, a * D:(a + 1) * D], w1t[:, k, a * D:(a + 1) * D], w2[:, k, :], start=k == 0, stop=k == 1)
            last.then_inc(s_pe0, 1)
            pe.wait_ge(s_bp, 2)
            pe.wait_ge(s_pchain, 1)

            def dense_turns(d):
                fixed = d.it is None
                first, second = (not fixed or 0 <= d.a - k < NC for k in range(2))
                if second:
                    pe.wait_ge(s_x3, at(d))
                    pe.wait_ge(s_xt, at(d))
                    turn(pt, x3).then_inc(s_tr, 1)
                if first:
                    pe.wait_ge(s_x1, at(d + 1))
                    pe.wait_ge(s_rt, at(d))
                    turn(pt, x1).then_inc(s_tx, 1)

            def dense_products(d):
                fixed = d.it is None
                first, second = (not fixed or 0 <= d.a - k < NC for k in range(2))
                if second:
                    pe.wait_ge(s_rt, at(d))
                    pe.wait_ge(s_ln, at(d + 1))
                    for t in range(NT):
                        biased(po[t], 2 + t)
                        last = product(po[t], lambda j: rt[:, j, :], wnt[:, 0, t, :])
                    last.then_inc(s_o, 1)
                if first:
                    pe.wait_ge(s_xt, at(d + 1))
                    biased(pz, 0)
                    product(pz, lambda j: xt[:, j, :], wab[:, 0, :]).then_inc(s_z, 1)

            def layer0(c):
                b, q = c.parity(), ph[0]
                d0, d1 = dense_of(0, c)
                pe.wait_ge(q["g"][b], at(counted(c, 32 * T)))
                pe.wait_ge(q["vA"], at(c))
                turn(pa, xs[b]).then_inc(q["tS"], 1)
                pe.wait_ge(q["vN"], at(c))
                turn(pb, xd[b]).then_inc(q["tD"], 1)
                dense_turns(d0)
                pe.wait_ge(q["aux"][b], at(counted(c, 64)))
                pe.wait_ge(q["eS"], at(c + 1))
                pe.wait_ge(q["vE"], at(c))
                mm(pc[:, 0:C], ks[:, :], stf, start=True, stop=False)
                mm(pc[:, 0:C], es[:, :], ea[b][:, :], start=False, stop=False)
                pe.wait_ge(q["eD"], at(c + 1))
                mm(pc[:, 0:C], qs[:, :], dtf, start=False, stop=True).then_inc(q["pA"], 1)
                mm(pa[:, 0:C], wv[:, :], stf, start=True, stop=True).then_inc(q["pB"], 1)
                dense_products(d0)
                dense_turns(d1)
                dense_products(d1)
                pe.wait_ge(q["vA"], at(c + 1))
                biased(pb, 1)
                product(pb, lambda j: agg[:, :, j], ident[:, :]).then_inc(q["pR"], 1)

            def layer1(c):
                b, q = c.parity(), ph[1]
                pe.wait_ge(q["g"][b], at(counted(c, 16 * T)))
                pe.wait_ge(q["aux"][b], at(counted(c, 32)))
                pe.wait_ge(q["vN"], at(c))
                pe.wait_ge(q["vA"], at(c))
                turn(pa, xs[b]).then_inc(q["tS"], 1)
                turn(pb, xd[b]).then_inc(q["tD"], 1)
                d = dense_of(1, c)[0]
                dense_turns(d)
                pe.wait_ge(q["eD"], at(c + 1))
                pe.wait_ge(q["eS"], at(c + 1))
                biased(pa, 0)
                product(pa, lambda j: st[:, :, j], wab[:, 0, :])
                biased(pb, 0)
                product(pb, lambda j: dt[:, :, j], wab[:, 0, :], stop=False)
                pe.wait_ge(q["vA"], at(c + 1))
                product(pb, lambda j: agg[:, :, j], wab[:, 1, :]).then_inc(q["pR"], 1)
                dense_products(d)

            def layer2(c):
                b, q = c.parity(), ph[2]
                pe.wait_ge(q["g"][b], at(counted(c, 16 * T)))
                pe.wait_ge(q["vN"], at(c))
                pe.wait_ge(q["vM"], at(c * REL))
                turn(pa, xs[b]).then_inc(q["tS"], 1)
                pe.wait_ge(q["vA"], at(c))
                for r in range(REL):
                    pe.wait_ge(q["vM"], at(c * REL + (r + 1)))
                    mm(pb[:, 0:C], wr[:, r, :], (wa, wb)[r % 2][:, :], start=r == 0, stop=r == REL - 1).then_inc(q["pM"], 1)
                d = dense_of(2, c)[0]
                dense_turns(d)
                dense_products(d)
                pe.wait_ge(q["vA"], at(c + 1))
                pe.wait_ge(q["eS"], at(c + 1))
                for j in range(T):
                    last = mm(pa[0:R, j * D:(j + 1) * D], run_tile(0, j), ident[:, :], start=True, stop=True)
                last.then_inc(q["pR"], 1)

            def layer3(c):
                b, q = c.parity(), ph[3]
                pe.wait_ge(q["g"][b], at(counted(c, 16 * T)))
                pe.wait_ge(q["aux"][b], at(counted(c, 48)))
                turn(bank[0], xs[b]).then_inc(q["tS"], 1)
                turn(bank[1], xd[b]).then_inc(q["tD"], 1)
                pe.wait_ge(q["eS"], at(c + 1))
                pe.wait_ge(q["eX"], at(c * NT))
                for t in range(NT):
                    mm(bank[2 + t][:, 0:C], ones_bf[0:1, :], off[b][0:1, t, :], start=True, stop=False)
                    mm(bank[2 + t][:, 0:C], wet[:, t, :], stf, start=False, stop=True).then_inc(q["pM"], 1)
                pe.wait_ge(q["eD"], at(c + 1))
                pe.wait_ge(q["vN"], at(c))
                for t in range(NT):
                    biased(bank[5 + t], 2 + t)
                    product(bank[5 + t], lambda j: dt[:, :, j], wnt[:, 0, t, :], stop=False)
                for k in range(NT):
                    pe.wait_ge(q["vA"], at(c * NT + (k + 1)))
                    for t in range(NT):
                        last = product(bank[5 + t], lambda j: run_tile(k, j), wnt[:, 1 + k, t, :], stop=k == NT - 1)
                last.then_inc(q["pR"], 1)

            for p, layer in enumerate((layer0, layer1, layer2, layer3)):
                over(pe, layer)
                if p == 2:
                    for d in (NC, NC + 1):
                        dense_turns(Lin(d))
                        dense_products(Lin(d))


def kernel(**inputs):
    import numpy as np
    import concourse.bacc as bacc
    from concourse.bass_utils import run_bass_kernel_spmd

    a = {k: np.asarray(v) for k, v in inputs.items()}
    W1, W2 = a["L1_gnn_W1"], a["L1_gnn_W2"]
    n, t = a["x"].shape[0], a["L3_gnn_W_e"].shape[0]
    laid = {
        "x": a["x"], "src": a["src"], "dst": a["dst"], "eattrT": a["edge_attr_64"].T,
        "etype3": a["edge_type_3"], "etype8": a["edge_type_8"][None], "eweight": a["edge_weight"][None],
        "ntype3": a["node_type_3"][:, None], "Wq": a["L0_gnn_Wq"], "Wk": a["L0_gnn_Wk"], "Wv": a["L0_gnn_Wv"],
        "We": a["L0_gnn_We"], "gate": a["L0_gnn_gate"], "bias0": a["L0_gnn_bias"][None],
        "W1T": W1.T.reshape(2, D, 2 * D).transpose(1, 0, 2), "b1": a["L1_gnn_b1"].reshape(2, D).T,
        "W2": W2.reshape(2, D, D).transpose(1, 0, 2), "b2": a["L1_gnn_b2"][None],
        "Wr": a["L2_gnn_weight"].transpose(1, 0, 2), "WeT": a["L3_gnn_W_e"].transpose(2, 0, 1),
        "beT": a["L3_gnn_b_e"].T, "WnT": a["L3_gnn_W_n"].reshape(t, D, 1 + t, D).transpose(3, 2, 0, 1),
        "bn": a["L3_gnn_b_n"], "ident": np.eye(D, dtype=np.float32),
    }
    nc = bacc.Bacc("TRN2", target_bir_lowering=False, num_devices=1)
    arrays, args = {}, []
    for name, v in laid.items():
        v = np.ascontiguousarray(v)
        arrays[f"in_{name}"] = v
        args.append(nc.dram_tensor(f"in_{name}", v.shape, mybir.dt.from_np(v.dtype), kind="ExternalInput").ap())
    args.append(nc.dram_tensor("out_rows", [n, D], F32, kind="ExternalOutput").ap())
    gnn_kernel(nc, *args)
    r = run_bass_kernel_spmd(nc, [arrays], core_ids=[0])
    return r.results[0]["out_rows"]
```

```python
from contextlib import ExitStack

import concourse.bass as bass
from concourse import mybir

F32 = mybir.dt.float32
BF16 = mybir.dt.bfloat16
I32 = mybir.dt.int32
ALU = mybir.AluOpType
ACT = mybir.ActivationFunctionType
AX_X = mybir.AxisListType.X

D = 128
R = 125
T = 4
C = R * T
EPS = 1e-5
TINY = 1e-16
BIG = 1e30
SKIP = 1 << 20
RSQRT_GUESS = 1597463007.0


class Lin:

    def __init__(self, a, s=0, it=None):
        self.a, self.s, self.it = a, s, it

    def __add__(self, n):
        return Lin(self.a + n, self.s, self.it)

    def __mul__(self, n):
        return Lin(self.a * n, self.s * n, self.it)

    def half(self):
        assert self.s % 2 == 0
        return Lin(self.a // 2, self.s // 2, self.it)

    def parity(self):
        return self.a % 2

    def v(self):
        return self.a if self.it is None or self.s == 0 else self.it * self.s + self.a


def at(count):
    if not isinstance(count, Lin):
        return max(count, 0)
    if count.it is None or count.s == 0:
        return max(count.a, 0)
    assert count.a > 0
    return count.v()


def settle(eng, sem):
    eng.sem_inc(sem, 1)


class Chain:

    def __init__(self, eng, sem):
        self.eng, self.sem, self.base, self.k, self.it, self.per = eng, sem, 0, 0, None, 0

    def step(self, ins):
        ins.then_inc(self.sem, 1)
        self.k += 1
        self.eng.wait_ge(self.sem, at(Lin(self.base + self.k, self.per, self.it)))

    def loop(self, it, per):
        self.base, self.k, self.it, self.per = self.base + self.k, 0, it, per

    def end(self, trips):
        assert self.k == self.per, f"{self.k} steps in the loop's body, {self.per} stated"
        self.base, self.k, self.it, self.per = self.base + trips * self.per, 0, None, 0


def gnn_kernel(nc, x, src, dst, eattrT, etype3, etype8, eweight, ntype3, Wq, Wk, Wv, We, gate,
               bias0, W1T, b1, W2, b2, Wr, WeT, beT, WnT, bn, ident_d, out):
    N, E = x.shape[0], src.shape[0]
    NC, EC = N // C, E // C
    PEEL, TAIL = 3, 4
    TR = (EC - PEEL - TAIL) // 2
    H = gate.shape[0]
    HC = D // H
    ED = eattrT.shape[0]
    REL = Wr.shape[1]
    NT = WeT.shape[1]
    INV = float(HC) ** -0.5
    PM = E // R
    assert N % C == 0 and E % C == 0 and (EC - PEEL - TAIL) % 2 == 0 and NC == 4 * EC

    rows = lambda a: a.rearrange("(n p j) d -> n p (j d)", p=R, j=T)
    x_c, out_c = rows(x), rows(out)
    src_c = src.rearrange("(n p j) -> n p j", p=R, j=T)
    dst_c = dst.rearrange("(n p j) -> n p j", p=R, j=T)
    nt_c = ntype3.rearrange("(n p j) o -> n p (j o)", p=R, j=T)

    s_rows = [nc.dram_tensor(f"source_rows{i}", [E, D], F32).ap() for i in (1, 2, 3)]
    d_rows = [nc.dram_tensor(f"target_rows{i}", [E, D], F32).ap() for i in (1, 2, 3)]
    same_d = nc.dram_tensor("same_d", [1, E], F32).ap()
    start_d = nc.dram_tensor("start_d", [1, E], F32).ap()
    deg_d = nc.dram_tensor("deg_d", [1, E], F32).ap()
    rdeg_d = nc.dram_tensor("rdeg_d", [1, E], F32).ap()
    last_d = nc.dram_tensor("last_d", [E], I32).ap()
    off_d = nc.dram_tensor("off_d", [NT, E], BF16).ap()
    slot_d = nc.dram_tensor("slot_d", [N, 1], I32).ap()
    last_c = last_d.rearrange("(n p j) -> n p j", p=R, j=T)

    ctx = ExitStack()
    with ctx:
        def sb(name, shape, dt=F32):
            return ctx.enter_context(nc.sbuf_tensor(name, shape, dt))

        def sem(name):
            return ctx.enter_context(nc.semaphore(name))

        def two(make, name, *a):
            return [make(f"{name}{i}", *a) for i in range(2)]

        wq, wk, wv = sb("wq", [D, D]), sb("wk", [D, D]), sb("wv", [D, D])
        qs, ks = sb("qs", [D, D]), sb("ks", [D, D])
        we, es = sb("we", [ED, D]), sb("es", [ED + 1, D])
        head = sb("head", [D, 3, H])
        gate_sb = sb("gate_sb", [ED + 1, H])
        w1t, w2 = sb("w1t", [D, 2, 2 * D]), sb("w2", [D, 2, D])
        b1c, b1m = sb("b1c", [D, 2]), sb("b1m", [D, 2, D])
        wab = sb("wab", [D, 2, D])
        wr, wet, wnt = sb("wr", [D, REL, D]), sb("wet", [D, NT, D]), sb("wnt", [D, 1 + NT, NT, D])
        bet = sb("bet", [D, NT])
        ident = sb("ident", [D, D])
        bias_bc = sb("bias_bc", [R, D])
        brow = sb("brow", [D, 2 + NT, D])
        b2row = sb("b2row", [D, D])
        brest = sb("brest", [D, 2 + NT, D])
        bhi, bmid, blo = (sb(n, [D, 2 + NT, D], BF16) for n in ("bhi", "bmid", "blo"))
        bparts = sb("bparts", [D, 2 + NT, T, D], BF16)
        ones_f = sb("ones_f", [D, 1])
        ones_bf = sb("ones_bf", [D, D], BF16)
        cur, prv, nxt = (sb(n, [R, PM], I32) for n in ("cur", "prv", "nxt"))
        ty = sb("ty", [R, PM], I32)
        same_p, start_p, more_p = (sb(n, [R, PM]) for n in ("same_p", "start_p", "more_p"))
        last_p = sb("last_p", [R, PM], I32)
        off_p = sb("off_p", [R, NT, PM], BF16)
        fill = sb("fill", [R, N // R], I32)
        eid = sb("eid", [R, EC, T], I32)
        slot_all, ntd_all = sb("slot_all", [R, EC, T], I32), sb("ntd_all", [R, EC, T], I32)
        xin, ntin = two(sb, "xin", [R, T, D]), two(sb, "ntin", [R, T], I32)
        y0 = two(sb, "y0_", [R, T, D])
        y1, sel = sb("y1", [R, T, D]), sb("sel", [R, T, D])
        x1, x3 = sb("x1", [R, T, D]), sb("x3", [R, T, D])
        xt = sb("xt", [D, T, R])
        rt = sb("rt", [D, T, R])
        res = two(sb, "res", [R, T, D])
        is_type = [two(sb, f"is_type{t}_", [R, T], I32) for t in range(1, NT)]
        G = 6
        bst = two(sb, "bst", [R, G * T, 6])
        msum, mdif, m2, ve, rst, nmr, tmp = (two(sb, n, [R, G * T]) for n in
                                             ("msum", "mdif", "m2_", "ve", "rst", "nmr", "tmp"))
        xs, xd = two(sb, "xs", [R, T, D]), two(sb, "xd", [R, T, D])
        isrc, idst, ilast, ieid = (two(sb, n, [R, T], I32) for n in ("isrc", "idst", "ilast", "ieid"))
        islot, intd = two(sb, "islot", [R, T], I32), two(sb, "intd", [R, T], I32)
        st, dt = sb("st", [D, R, T]), sb("dt", [D, R, T])
        stf, dtf = (a[:, :, :].rearrange("d p j -> d (p j)") for a in (st, dt))
        ea = two(sb, "ea", [ED + 1, C])
        same = two(sb, "same", [D, C])
        aux = two(sb, "aux", [D, C])
        rel = two(sb, "rel", [D, C], I32)
        off = two(sb, "off", [1, NT, C], BF16)
        rows_same = two(sb, "rows_same", [1, C])
        deg = two(sb, "deg", [1, C])
        degp = sb("degp", [R, PM])
        run, run2 = sb("run", [D, 3, C + 1]), sb("run2", [D, 3, C + 1])
        masked = sb("masked", [D, REL, C])
        den = sb("den", [R, T * H])
        headsel = sb("headsel", [D, H])
        wa, wb, wc = (masked[:, k, :] for k in range(3))
        agg = sb("agg", [D, R, T])
        aggf = agg[:, :, :].rearrange("d p j -> d (p j)")
        ys, yd = sb("ys", [R, T, D]), sb("yd", [R, T, D])
        so, so3, do = (two(sb, n, [R, T, D]) for n in ("so", "so3", "do"))
        ysb, xdb = so3, two(sb, "xdb", [R, T, D])

        bank = [ctx.enter_context(nc.psum_tensor(f"bank{i}", [D, 512], F32)) for i in range(8)]
        pt, pz, po = bank[0], bank[1], bank[2:5]
        pa, pb, pc = bank[5:8]

        s_w, s_idx, s_slotrow, s_prep, s_scr, s_pe0, s_bp, s_const = map(
            sem, ("s_w", "s_idx", "s_slotrow", "s_prep", "s_scr", "s_pe0", "s_bp", "s_const"))
        s_fill, s_passed, s_rdeg, s_rd, s_hs = map(sem, ("s_fill", "s_passed", "s_rdeg", "s_rd", "s_hs"))
        s_xin, s_res = two(sem, "s_xin"), two(sem, "s_res")
        s_y0, s_ln, s_x1, s_x3, s_out = map(sem, ("s_y0", "s_ln", "s_x1", "s_x3", "s_out"))
        s_tx, s_xt, s_z, s_tr, s_rt, s_o, s_sel = map(sem, ("s_tx", "s_xt", "s_z", "s_tr", "s_rt", "s_o", "s_sel"))
        s_chain, s_pchain, s_achain = sem("s_chain"), sem("s_pchain"), sem("s_achain")

        SINGLE = ("tS tD eS eD pA pB pR vA vE eX nS nD yb eN", "tS tD eS eD pR vA nS nD",
                  "tS eS pM pR vA vM nD", "tS tD eS eD pM pR vA eX vN nD sel")
        PAIRS = ("aux idx g stS stD sc dg", "ld aux ix g gi stS stD", "ld aux rl ix g gi stD", "ld aux g sc")

        ph = [{**{k: sem(f"layer{n}_{k}") for k in SINGLE[n].split()},
               **{k: two(sem, f"layer{n}_{k}_") for k in PAIRS[n].split()}} for n in range(4)]

        def counted(chunk, per):
            return (chunk.half() + 1) * per

        def over(eng, body, chain=None, per=0):
            for c in range(PEEL):
                body(Lin(c))
            with eng.Fori(0, TR) as it:
                if chain:
                    chain.loop(it, per)
                body(Lin(PEEL, 2, it))
                body(Lin(PEEL + 1, 2, it))
            if chain:
                chain.end(TR)
            for c in range(EC - TAIL, EC):
                body(Lin(c))

        def there(c):
            return c.it is not None or c.a < EC

        def dense_of(p, c):
            if p == 0:
                return [c * 2, c * 2 + 1]
            return [c + (2 * EC if p == 1 else 3 * EC)] if p < 3 else []

        def block_of(p, c):
            return dense_of(p, c)[-1]

        NLOADS = 16 + NT
        DVE_STEPS = (92, 42, 40, 38)
        POOL_STEPS = (2, 2, 4, 2)
        one_row = ones_f[0:1, 0:1].broadcast_to([1, C])
        run_tile = lambda m, k, j: m[:, k, 1:C + 1].rearrange("d (p j) -> d p j", j=T)[:, :, j]
        block = ctx.enter_context(nc.Block())

        @block.sync
        def _(sp):
            pm = lambda a: a.rearrange("(p t) -> p t", t=PM)
            sp.wait_ge(s_const, 1)
            sp.dma_start(cur[:, :], pm(dst)).then_inc(s_idx, 16)
            sp.dma_start(prv[1:R, :], bass.AP(dst.tensor, PM - 1, [[PM, R - 1], [1, PM]])).then_inc(s_idx, 16)
            sp.dma_start(prv[0:1, 1:PM], bass.AP(dst.tensor, 0, [[PM, 1], [1, PM - 1]])).then_inc(s_idx, 16)
            sp.dma_start(nxt[0:R - 1, :], bass.AP(dst.tensor, 1, [[PM, R - 1], [1, PM]])).then_inc(s_idx, 16)
            sp.dma_start(nxt[R - 1:R, 0:PM - 1], bass.AP(dst.tensor, E - PM + 1, [[PM, 1], [1, PM - 1]])).then_inc(s_idx, 16)
            sp.dma_start(ty[:, :], pm(etype3)).then_inc(s_idx, 16)
            loads = [(ident[:, :], ident_d), (bias_bc[:, :], bias0[0:1, :].broadcast_to([R, D])),
                     (wq[:, :], Wq), (wk[:, :], Wk), (wv[:, :], Wv), (we[:, :], We),
                     (gate_sb[ED:ED + 1, :], gate[None, :]), (w1t[:, :, :], W1T), (w2[:, :, :], W2),
                     (b1c[:, :], b1), (b2row[:, :], b2[0:1, :].broadcast_to([D, D])),
                     (brow[:, 1, :], bias0[0:1, :].broadcast_to([D, D])),
                     (wr[:, :, :], Wr), (wet[:, :, :], WeT), (wnt[:, :, :, :], WnT), (bet[:, :], beT)]
            loads += [(brow[:, 2 + t, :], bn[t:t + 1, :].broadcast_to([D, D])) for t in range(NT)]
            for to, of in loads:
                sp.dma_start(to, of).then_inc(s_w, 16)
            sp.wait_ge(s_prep, 1)
            sp.wait_ge(s_fill, 1)
            row = lambda a: a.rearrange("o (p t) -> (o p) t", t=PM)
            sp.dma_start(slot_d.rearrange("(p t) o -> p (t o)", p=R), fill[:, :]).then_inc(s_slotrow, 16)
            sp.dma_start(row(same_d), same_p[:, :]).then_inc(s_scr, 16)
            sp.dma_start(row(start_d), start_p[:, :]).then_inc(s_scr, 16)
            sp.dma_start(pm(last_d), last_p[:, :]).then_inc(s_scr, 16)
            for t in range(NT):
                sp.dma_start(off_d[t].rearrange("(p t) -> p t", t=PM), off_p[:, t, :]).then_inc(s_scr, 16)
            sp.wait_ge(s_scr, 16 * (3 + NT))

            flat = lambda a: a[:, :, :].rearrange("p j d -> p (j d)")
            cols = lambda c: bass.ds(c.v() * C, C)
            to_all = lambda a, c: a[0:1, cols(c)].broadcast_to([D, C])

            def load_dense(d):
                b = d.parity()
                sp.wait_ge(s_y0, at(d + (-1)))
                sp.wait_ge(s_ln, at(d + (-1)))
                sp.dma_start(flat(xin[b]), x_c[d.v()]).then_inc(s_xin[b], 16)
                sp.dma_start(ntin[b][:, :], nt_c[d.v()]).then_inc(s_xin[b], 16)

            def store_dense(d):
                b = d.parity()
                sp.wait_ge(s_out, at(d + 1))
                sp.dma_start(out_c[d.v()], flat(res[b])).then_inc(s_res[b], 16)

            def indices0(c):
                b, q = c.parity(), ph[0]
                sp.wait_ge(q["g"][b], at(c.half() * (32 * T)))
                settle(sp, s_passed)
                sp.wait_ge(q["sc"][b], at(c.half() * (16 * T)))
                sp.dma_start(isrc[b][:, :], src_c[c.v()]).then_inc(q["idx"][b], 16)
                sp.dma_start(idst[b][:, :], dst_c[c.v()]).then_inc(q["idx"][b], 16)
                sp.dma_start(ilast[b][:, :], last_c[c.v()]).then_inc(q["idx"][b], 16)

            def features0(c):
                b, q = c.parity(), ph[0]
                sp.wait_ge(q["vA"], at(c + (-1)))
                sp.dma_start(ea[b][0:ED, :], eattrT[:, cols(c)]).then_inc(q["aux"][b], 16)
                sp.dma_start(ea[b][ED:ED + 1, :], eweight[0:1, cols(c)]).then_inc(q["aux"][b], 16)
                sp.dma_start(rows_same[b][:, :], same_d[0:1, cols(c)]).then_inc(q["aux"][b], 16)
                sp.dma_start(aux[b][:, :], to_all(start_d, c)).then_inc(q["aux"][b], 16)

            def store0(c):
                b, q = c.parity(), ph[0]
                sp.wait_ge(q["vA"], at(c + 1))
                sp.dma_start(deg_d[0:1, cols(c)], deg[b][:, :]).then_inc(q["dg"][b], 16)
                sp.wait_ge(q["nS"], at(c + 1))
                sp.dma_start(rows(s_rows[0])[c.v()], flat(so[b])).then_inc(q["stS"][b], 16)
                sp.wait_ge(q["nD"], at(c + 1))
                sp.dma_start(rows(d_rows[0])[c.v()], flat(do[b])).then_inc(q["stD"][b], 16)

            def indices1(c):
                b, q = c.parity(), ph[1]
                sp.wait_ge(q["gi"][b], at(c.half() * (16 * T)))
                sp.dma_start(isrc[b][:, :], src_c[c.v()]).then_inc(q["ix"][b], 16)

            def rows1(c):
                b, q = c.parity(), ph[1]
                if c.it is not None or c.a >= 2:
                    sp.wait_ge(s_ln, at(block_of(1, c) + (-1)))
                sp.dma_start(flat(xs[b]), rows(s_rows[0])[c.v()]).then_inc(q["ld"][b], 16)
                sp.dma_start(flat(xd[b]), rows(d_rows[0])[c.v()]).then_inc(q["aux"][b], 16)
                sp.dma_start(same[b][:, :], to_all(same_d, c)).then_inc(q["aux"][b], 16)
                sp.dma_start(aux[b][:, :], to_all(rdeg_d, c)).then_inc(q["aux"][b], 16)

            def store1(c):
                b, q = c.parity(), ph[1]
                sp.wait_ge(q["nS"], at(c + 1))
                sp.dma_start(rows(s_rows[1])[c.v()], flat(so[b])).then_inc(q["stS"][b], 16)
                sp.dma_start(rows(s_rows[2])[c.v()], flat(so3[b])).then_inc(q["stS"][b], 16)
                sp.wait_ge(q["nD"], at(c + 1))
                sp.dma_start(rows(d_rows[1])[c.v()], flat(do[b])).then_inc(q["stD"][b], 16)

            def indices2(c):
                b, q = c.parity(), ph[2]
                sp.wait_ge(q["gi"][b], at(c.half() * (16 * T)))
                sp.dma_start(idst[b][:, :], dst_c[c.v()]).then_inc(q["ix"][b], 16)

            def sources2(c):
                b, q = c.parity(), ph[2]
                sp.wait_ge(q["tS"], at(c + (-1)))
                sp.dma_start(flat(xs[b]), rows(s_rows[1])[c.v()]).then_inc(q["ld"][b], 16)

            def relations2(c):
                b, q = c.parity(), ph[2]
                sp.wait_ge(q["vM"], at((c + (-1)) * REL))
                sp.dma_start(rel[b][:, :], to_all(etype8, c)).then_inc(q["rl"][b], 16)

            def targets2(c):
                b, q = c.parity(), ph[2]
                if c.it is not None or c.a >= 2:
                    sp.wait_ge(s_ln, at(block_of(2, c) + (-1)))
                sp.dma_start(flat(xd[b]), rows(d_rows[1])[c.v()]).then_inc(q["aux"][b], 16)
                sp.dma_start(same[b][:, :], to_all(same_d, c)).then_inc(q["aux"][b], 16)

            def store2(c):
                b, q = c.parity(), ph[2]
                sp.wait_ge(q["nD"], at(c + 1))
                sp.dma_start(rows(d_rows[2])[c.v()], flat(do[b])).then_inc(q["stD"][b], 16)

            def sources3(c):
                b, q = c.parity(), ph[3]
                sp.wait_ge(q["tS"], at(c + (-1)))
                settle(sp, s_passed)
                sp.wait_ge(q["pM"], at((c + (-1)) * NT))
                sp.dma_start(flat(xs[b]), rows(s_rows[2])[c.v()]).then_inc(q["ld"][b], 16)
                sp.dma_start(off[b][:, :, :], off_d[:, cols(c)][None]).then_inc(q["ld"][b], 16)

            def targets3(c):
                b, q = c.parity(), ph[3]
                sp.wait_ge(q["vN"], at(c + (-1)))
                sp.wait_ge(q["sc"][b], at(c.half() * (16 * T)))
                sp.dma_start(flat(xd[b]), rows(d_rows[2])[c.v()]).then_inc(q["aux"][b], 16)
                sp.dma_start(same[b][:, :], to_all(same_d, c)).then_inc(q["aux"][b], 16)
                sp.dma_start(ilast[b][:, :], last_c[c.v()]).then_inc(q["aux"][b], 16)

            def stored(p):
                for b in range(2):
                    n = (EC + 1 - b) // 2
                    if p < 2:
                        sp.wait_ge(ph[p]["stS"][b], (1 + p) * 16 * n)
                    if p == 0:
                        sp.wait_ge(ph[p]["dg"][b], 16 * n)
                    sp.wait_ge(ph[p]["stD"][b], 16 * n)

            plan = (((indices0, 2), (features0, 2)), ((indices1, 3), (rows1, 1)),
                    ((sources2, 3), (indices2, 1), (relations2, 2), (targets2, 1)), ((sources3, 2), (targets3, 1)))
            stores = (store0, store1, store2, None)
            load_dense(Lin(0))
            for p in range(4):
                if p:
                    stored(p - 1)
                if p == 1:
                    sp.dma_start(degp[:, :], deg_d.rearrange("o (p t) -> (o p) t", t=PM)).then_inc(s_rdeg, 16)
                    sp.wait_ge(s_rd, 1)
                    sp.dma_start(rdeg_d.rearrange("o (p t) -> (o p) t", t=PM), degp[:, :]).then_inc(s_rdeg, 16)
                    sp.wait_ge(s_rdeg, 32)
                for load, ahead in plan[p]:
                    for c in range(ahead):
                        load(Lin(c))

                def body(c):
                    for load, ahead in plan[p]:
                        if there(c + ahead):
                            load(c + ahead)
                    for d in dense_of(p, c):
                        if d.it is not None or d.a + 1 < NC:
                            load_dense(d + 1)
                        if d.it is not None or d.a >= 2:
                            store_dense(d + (-2))
                    if stores[p] and (c.it is not None or c.a >= 1):
                        stores[p](c + (-1))

                over(sp, body)
                if stores[p]:
                    stores[p](Lin(EC - 1))
                if p == 2:
                    for d in range(NC - 2, NC):
                        store_dense(Lin(d))

        bc = lambda a: a.unsqueeze(2).broadcast_to([R, T, D])
        tile_of = lambda a, j: a[:, j * R:(j + 1) * R]
        flat_bank = lambda k: k[0:R, 0:T * D].rearrange("p (j d) -> p j d", j=T)
        by_tile = lambda k: k[:, 0:C].rearrange("d (j p) -> d j p", j=T)
        bias_rows = bias_bc[:, :].unsqueeze(1).broadcast_to([R, T, D])

        @block.gpsimd
        def _(pool):
            chain = Chain(pool, s_pchain)
            nc.gpsimd.memset(prv[:, :], -1)
            nc.gpsimd.memset(nxt[:, :], -1).then_inc(s_const, 1)
            nc.gpsimd.memset(fill[:, :], SKIP).then_inc(s_fill, 1)
            nc.gpsimd.iota(eid[:, :, :], pattern=[[C, EC], [1, T]], base=0, channel_multiplier=T)
            nc.gpsimd.memset(ones_f[:, :], 1.0)
            chain.step(nc.gpsimd.memset(ones_bf[:, :], 1.0))

            def gather(to, table, index, j, bound):
                if j == 0:
                    settle(pool, s_passed)
                return nc.gpsimd.indirect_dma_start(
                    out=to, out_offset=None, in_=table,
                    in_offset=bass.IndirectOffsetOnAxis(ap=index[:, j:j + 1], axis=0),
                    bounds_check=bound, oob_is_err=False)

            def scatter(table, index, j, of):
                if j == 0:
                    settle(pool, s_passed)
                return nc.gpsimd.indirect_dma_start(
                    out=table, out_offset=bass.IndirectOffsetOnAxis(ap=index[:, j:j + 1], axis=0),
                    in_=of, in_offset=None, bounds_check=N - 1, oob_is_err=False)

            def add_bias(d):
                b = d.parity()
                pool.wait_ge(s_xin[b], at(counted(d, 32)))
                pool.wait_ge(s_x1, at(d + (-1)))
                nc.gpsimd.tensor_tensor(y0[b][:, :, :], xin[b][:, :, :], bias_rows, ALU.add).then_inc(s_y0, 1)

            def rows0(c):
                b, q = c.parity(), ph[0]
                pool.wait_ge(q["idx"][b], at(counted(c, 48)))
                pool.wait_ge(q["tD"], at(c + (-1)))
                for j in range(T):
                    gather(xs[b][:, j, :], x, isrc[b], j, N - 1).then_inc(q["g"][b], 16)
                    gather(xd[b][:, j, :], x, idst[b], j, N - 1).then_inc(q["g"][b], 16)

            def marks0(c):
                b, q = c.parity(), ph[0]
                chain.step(nc.gpsimd.tensor_copy(ieid[b][:, :], eid[:, c.v(), :]))
                if c.it is None and c.a == 0:
                    pool.wait_ge(s_slotrow, 16)
                for j in range(T):
                    scatter(slot_d, ilast[b], j, ieid[b][:, j:j + 1]).then_inc(q["sc"][b], 16)
                pool.wait_ge(q["g"][b], at(counted(c, 32 * T)))
                pool.wait_ge(q["nD"], at(c + (-1)))
                nc.gpsimd.tensor_tensor(ysb[b][:, :, :], xs[b][:, :, :], bias_rows, ALU.add)
                nc.gpsimd.tensor_tensor(xdb[b][:, :, :], xd[b][:, :, :], bias_rows, ALU.add).then_inc(q["yb"], 1)

            def layer0(c):
                d0, d1 = dense_of(0, c)
                add_bias(d0)
                if there(c + 1):
                    rows0(c + 1)
                add_bias(d1)
                if there(c + 1):
                    marks0(c + 1)

            def slots1(c):
                b, q = c.parity(), ph[1]
                pool.wait_ge(q["ix"][b], at(counted(c, 16)))
                pool.wait_ge(q["g"][b], at(c.half() * (16 * T)))
                for j in range(T):
                    gather(islot[b][:, j:j + 1], slot_d, isrc[b], j, N - 1).then_inc(q["gi"][b], 16)

            def rows1(c):
                b, q = c.parity(), ph[1]
                pool.wait_ge(q["gi"][b], at(counted(c, 16 * T)))
                pool.wait_ge(q["ld"][b], at(counted(c, 16)))
                for j in range(T):
                    gather(xs[b][:, j, :], d_rows[0], islot[b], j, E - 1).then_inc(q["g"][b], 16)
                chain.step(nc.gpsimd.tensor_copy(slot_all[:, c.v(), :], islot[b][:, :]))
                settle(pool, s_passed)

            def layer1(c):
                add_bias(dense_of(1, c)[0])
                if there(c + 1):
                    rows1(c + 1)
                if there(c + 2):
                    slots1(c + 2)

            def updated(p, c):
                b, q = c.parity(), ph[p]
                pool.wait_ge(q["g"][b], at(c.half() * (16 * T)))
                settle(pool, s_passed)
                chain.step(nc.gpsimd.tensor_copy(islot[b][:, :], slot_all[:, c.v(), :]))
                pool.wait_ge(q["ld"][b], at(counted(c, 16 if p == 2 else 32)))
                for j in range(T):
                    gather(xs[b][:, j, :], d_rows[p - 1], islot[b], j, E - 1).then_inc(q["g"][b], 16)

            def types2(c):
                b, q = c.parity(), ph[2]
                pool.wait_ge(q["ix"][b], at(counted(c, 16)))
                for j in range(T):
                    gather(intd[b][:, j:j + 1], ntype3, idst[b], j, N - 1).then_inc(q["gi"][b], 16)
                pool.wait_ge(q["gi"][b], at(counted(c, 16 * T)))
                settle(pool, s_passed)
                chain.step(nc.gpsimd.tensor_copy(ntd_all[:, c.v(), :], intd[b][:, :]))
                settle(pool, s_passed)

            def layer2(c):
                add_bias(dense_of(2, c)[0])
                if there(c + 2):
                    updated(2, c + 2)
                types2(c)

            def layer3(c):
                b, q = c.parity(), ph[3]
                if there(c + 2):
                    updated(3, c + 2)
                if c.it is None and c.a == 0:
                    for k in range(2):
                        pool.wait_ge(s_res[k], 16 * (NC // 2))
                pool.wait_ge(q["nD"], at(c + 1))
                pool.wait_ge(q["aux"][b], at(counted(c, 48)))
                for j in range(T):
                    scatter(out, ilast[b], j, do[b][:, j, :]).then_inc(q["sc"][b], 16)

            def landed(p):
                for b in range(2):
                    n = (EC + 1 - b) // 2
                    if p == 1:
                        pool.wait_ge(ph[0]["sc"][b], 16 * T * n)
                    pool.wait_ge(ph[p - 1]["stD"][b], 16 * n)
                    pool.wait_ge(ph[p - 1]["g"][b], (32 if p == 1 else 16) * T * n)

            rows0(Lin(0))
            marks0(Lin(0))
            over(pool, layer0, chain, POOL_STEPS[0])
            landed(1)
            slots1(Lin(0))
            rows1(Lin(0))
            slots1(Lin(1))
            over(pool, layer1, chain, POOL_STEPS[1])
            for p, layer in ((2, layer2), (3, layer3)):
                landed(p)
                updated(p, Lin(0))
                updated(p, Lin(1))
                over(pool, layer, chain, POOL_STEPS[p])
            for b in range(2):
                pool.wait_ge(ph[3]["sc"][b], 16 * T * ((EC + 1 - b) // 2))

        @block.vector
        def _(dve):
            V = nc.vector
            chain = Chain(dve, s_chain)
            step = chain.step
            dve.wait_ge(s_idx, 96)
            V.tensor_tensor(same_p[:, :], cur[:, :], prv[:, :], ALU.is_equal)
            V.tensor_tensor(more_p[:, :], cur[:, :], nxt[:, :], ALU.is_equal)
            for t in range(NT):
                V.tensor_scalar(off_p[:, t, :], ty[:, :], t, -BIG, ALU.not_equal, ALU.mult)
            step(V.memset(run[:, :, :], 0.0))
            V.tensor_scalar(start_p[:, :], same_p[:, :], -1.0, BIG, ALU.add, ALU.mult)
            V.scalar_tensor_tensor(out=last_p[:, :], in0=more_p[:, :], scalar=float(SKIP), in1=cur[:, :],
                                   op0=ALU.mult, op1=ALU.add).then_inc(s_prep, 1)
            dve.wait_ge(s_w, 16 * NLOADS)
            for i, w in enumerate((wq, wk)):
                V.tensor_reduce(head[:, i, :], w[:, :].rearrange("k (h c) -> k h c", h=H), AX_X, ALU.add)
            V.tensor_reduce(head[0:ED, 2, :], we[:, :].rearrange("k (h c) -> k h c", h=H), AX_X, ALU.add)
            V.tensor_copy(b1m[:, :, :], b1c[:, :].unsqueeze(2).broadcast_to([D, 2, D]))
            step(V.memset(bparts[:, :, :, :], 0.0))
            heads = lambda a, n: a.unsqueeze(2).broadcast_to([n, H, HC])
            for i, w in enumerate((qs, ks)):
                V.tensor_scalar(w[:, :].rearrange("k (h c) -> k h c", h=H), heads(head[:, i, :], D), INV, None, ALU.mult)
            V.tensor_scalar(es[0:ED, :].rearrange("k (h c) -> k h c", h=H), heads(head[0:ED, 2, :], ED), INV, None, ALU.mult)
            V.tensor_copy(es[ED:ED + 1, :].rearrange("k (h c) -> k h c", h=H),
                          heads(gate_sb[ED:ED + 1, :], 1)).then_inc(s_bp, 1)
            dve.wait_ge(s_pe0, 1)
            V.tensor_copy(wab[:, :, :], bank[1][:, 0:2 * D].rearrange("k (a d) -> k a d", a=2))
            step(V.tensor_tensor(brow[:, 0, :], bank[0][:, 0:D], b2row[:, :], ALU.add))
            step(V.tensor_copy(bhi[:, :, :], brow[:, :, :]))
            step(V.tensor_tensor(brest[:, :, :], brow[:, :, :], bhi[:, :, :], ALU.subtract))
            step(V.tensor_copy(bmid[:, :, :], brest[:, :, :]))
            step(V.tensor_tensor(brest[:, :, :], brest[:, :, :], bmid[:, :, :], ALU.subtract))
            step(V.tensor_copy(blo[:, :, :], brest[:, :, :]))
            for part, p in ((bhi, 0), (bmid, 32), (blo, 64)):
                for j in range(T):
                    last = V.tensor_copy(bparts[p:p + 1, :, j, :], part[p:p + 1, :, :])
            last.then_inc(s_bp, 1)

            V.tensor_copy(headsel[:, :], ident[:, :].rearrange("k (h c) -> k h c", h=H)[:, :, 0]).then_inc(s_hs, 1)

            def stats(y, s, g):
                for j in range(T):
                    last = V.bn_stats(bst[s][:, g * T + j, :], y[:, j, :])
                return last

            def rsqrt(s, lo, hi, twice, done):
                g = slice(lo * T, hi * T)
                b_, ms, md, m, v, r, t = (a[s] for a in (bst, msum, mdif, m2, ve, rst, tmp))
                V.tensor_tensor(md[:, g], b_[:, g, 1], b_[:, g, 4], ALU.subtract)
                V.tensor_tensor(ms[:, g], b_[:, g, 1], b_[:, g, 4], ALU.add)
                step(V.tensor_tensor(m[:, g], b_[:, g, 2], b_[:, g, 5], ALU.add))
                step(V.tensor_tensor(md[:, g], md[:, g], md[:, g], ALU.mult))
                step(V.scalar_tensor_tensor(out=m[:, g], in0=md[:, g], scalar=D / 4.0, in1=m[:, g], op0=ALU.mult, op1=ALU.add))
                for k in range(lo, hi):
                    a = slice(k * T, (k + 1) * T)
                    if k in twice:
                        last = V.tensor_scalar(v[:, a], m[:, a], (1.0 + EPS) / D, EPS * EPS, ALU.mult, ALU.add)
                    elif k == lo or k - 1 in twice:
                        e = min([x for x in twice if x > k] + [hi])
                        a = slice(k * T, e * T)
                        last = V.tensor_scalar(v[:, a], m[:, a], 1.0 / D, EPS, ALU.mult, ALU.add)
                step(last)
                step(V.tensor_scalar(r[:, g].bitcast(I32), v[:, g].bitcast(I32), -0.5, RSQRT_GUESS, ALU.mult, ALU.add))
                for _ in range(3):
                    step(V.scalar_tensor_tensor(out=t[:, g], in0=r[:, g], scalar=-0.5, in1=r[:, g], op0=ALU.mult, op1=ALU.mult))
                    step(V.tensor_tensor(t[:, g], t[:, g], v[:, g], ALU.mult))
                    step(V.scalar_tensor_tensor(out=r[:, g], in0=t[:, g], scalar=1.5, in1=r[:, g], op0=ALU.add, op1=ALU.mult))
                V.scalar_tensor_tensor(out=nmr[s][:, g], in0=ms[:, g], scalar=-0.5, in1=r[:, g],
                                       op0=ALU.mult, op1=ALU.mult).then_inc(done, 1)

            def dense(d, edges=None, extra=(), twice=(1,)):
                fixed = d.it is None
                first, second, third = (not fixed or 0 <= d.a - k < NC for k in range(3))
                s = d.parity()
                b = s
                if third:
                    dve.wait_ge(s_sel, at(d + (-1)))
                    settle(dve, s_passed)
                    step(V.copy_predicated(sel[:, :, :], bc(is_type[0][b][:, :]), flat_bank(po[1])))
                if second:
                    dve.wait_ge(s_z, at(d))
                    dve.wait_ge(s_x3, at(d + (-1)))
                    V.scalar_tensor_tensor(out=y1[:, :, :], in0=flat_bank(pz), scalar=0.0, in1=x1[:, :, :],
                                           op0=ALU.max, op1=ALU.add)
                if third:
                    settle(dve, s_passed)
                    step(V.copy_predicated(sel[:, :, :], bc(is_type[1][b][:, :]), flat_bank(po[2])))
                    V.scalar_tensor_tensor(out=sel[:, :, :], in0=x3[:, :, :], scalar=2.0, in1=sel[:, :, :],
                                           op0=ALU.mult, op1=ALU.add)
                if first:
                    dve.wait_ge(s_xin[b], at(counted(d, 32)))
                    for t in range(1, NT):
                        last = V.tensor_scalar(is_type[t - 1][b][:, :], ntin[b][:, :], t, None, ALU.is_equal)
                    step(last)
                else:
                    step(V.memset(tmp[s][0:1, 0:1], 0.0))
                dve.wait_ge(s_x1, at(d + (-1)) if not fixed else min(max(d.a - 1, 0), NC))
                if first:
                    dve.wait_ge(s_y0, at(d + 1))
                    stats(y0[b], s, 2)
                if second:
                    stats(y1, s, 1)
                if third:
                    stats(sel, s, 0)
                if edges:
                    edges()
                for y, g in extra:
                    stats(y, s, g)
                step(V.memset(tmp[s][0:1, 0:1], 0.0))
                lo = 0 if third else 1 if second else 2
                hi = extra[-1][1] + 1 if extra else 3 if first else 2 if second else 1
                rsqrt(s, lo, hi, twice, s_ln)

            def scan(m, k, data0, data1, op0, op1, start=None):
                return V.tensor_tensor_scan(m[:, k, 1:C + 1], data0, data1, m[:, k, 0:1] if start is None else start, op0, op1)

            carry = lambda n: V.tensor_copy(run[:, 0:n, 0:1], run[:, 0:n, C:C + 1])

            def scores(c):
                b, q = c.parity(), ph[0]
                dve.wait_ge(q["pA"], at(c + 1))
                dve.wait_ge(q["aux"][b], at(counted(c, 64)))
                dve.wait_ge(q["vA"], at(c))
                step(V.tensor_scalar(wc, pc[:, 0:C], 0.2, None, ALU.mult))
                step(V.tensor_tensor(wa, wc, pc[:, 0:C], ALU.max))
                step(scan(run, 0, aux[b][:, :], wa, ALU.add, ALU.max))
                step(V.tensor_tensor(wb, run[:, 0, 0:C], aux[b][:, :], ALU.add))
                V.tensor_tensor(wa, wa, run[:, 0, 1:C + 1], ALU.subtract)
                V.tensor_tensor(wb, wb, run[:, 0, 1:C + 1], ALU.subtract).then_inc(q["vE"], 1)

            def sums(c):
                b, q = c.parity(), ph[0]
                dve.wait_ge(q["eX"], at(c + 1))
                dve.wait_ge(q["pB"], at(c + 1))
                dve.wait_ge(q["dg"][b], at(c.half() * 16))
                dve.wait_ge(q["pR"], at(c))
                V.tensor_tensor_scan(deg[b][:, :], rows_same[b][:, :], one_row,
                                     0.0 if c.it is None and c.a == 0 else deg[1 - b][:, C - 1:C], ALU.mult, ALU.add)
                scan(run, 2, wb, wa, ALU.mult, ALU.add)
                step(V.tensor_tensor(wc, pa[:, 0:C], wa, ALU.mult))
                scan(run, 1, wb, wc, ALU.mult, ALU.add).then_inc(q["vA"], 1)
                dve.wait_ge(q["vA"], at(c + 1))
                step(carry(3))

            def layer0(c):
                b, q = c.parity(), ph[0]
                d0, d1 = dense_of(0, c)
                scores(c)

                def source_rows():
                    dve.wait_ge(q["yb"], at(c + 1))

                def target_rows():
                    dve.wait_ge(q["pR"], at(c + 1))
                    dve.wait_ge(q["yb"], at(c + 1))
                    dve.wait_ge(q["nD"], at(c))
                    dve.wait_ge(q["eN"], at(c + 1))
                    step(V.tensor_scalar(den[:, :], den[:, :], TINY, None, ALU.add))
                    step(V.reciprocal(den[:, :], den[:, :]))
                    step(V.tensor_tensor(yd[:, :, :].rearrange("p j (h k) -> p (j h) k", h=H),
                                         pb[0:R, 0:T * D].rearrange("p (g k) -> p g k", k=HC),
                                         den[:, :].unsqueeze(2).broadcast_to([R, T * H, HC]), ALU.mult))
                    step(V.tensor_tensor(yd[:, :, :], yd[:, :, :], xdb[b][:, :, :], ALU.add))

                dense(d0, source_rows, ((ysb[b], 3),))
                sums(c)
                dense(d1, target_rows, ((yd, 3),))

            def layer1(c):
                b, q = c.parity(), ph[1]
                dve.wait_ge(q["eS"], at(c + 1))
                dve.wait_ge(q["aux"][b], at(counted(c, 48)))
                dve.wait_ge(q["pR"], at(c))
                step(scan(run, 0, same[b][:, :], stf, ALU.mult, ALU.add))
                V.tensor_tensor(aggf, run[:, 0, 1:C + 1], aux[b][:, :], ALU.mult).then_inc(q["vA"], 1)
                step(carry(1))

                def edge_rows():
                    dve.wait_ge(q["pR"], at(c + 1))
                    dve.wait_ge(q["nS"], at(c))
                    dve.wait_ge(q["nD"], at(c))
                    V.scalar_tensor_tensor(out=ys[:, :, :], in0=flat_bank(pa), scalar=0.0, in1=xs[b][:, :, :],
                                           op0=ALU.max, op1=ALU.add)
                    step(V.scalar_tensor_tensor(out=yd[:, :, :], in0=flat_bank(pb), scalar=0.0, in1=xd[b][:, :, :],
                                                op0=ALU.max, op1=ALU.add))

                dense(dense_of(1, c)[0], edge_rows, ((ys, 3), (ys, 4), (yd, 5)), (1, 4))

            def masks(c):
                b, q = c.parity(), ph[2]
                dve.wait_ge(q["eS"], at(c + 1))
                dve.wait_ge(q["rl"][b], at(counted(c, 16)))
                dve.wait_ge(q["pM"], at(c * REL))
                for r in range(REL):
                    V.scalar_tensor_tensor(out=masked[:, r, :], in0=rel[b][:, :], scalar=float(r), in1=stf,
                                           op0=ALU.is_equal, op1=ALU.mult).then_inc(q["vM"], 1)

            def layer2(c):
                b, q = c.parity(), ph[2]
                dve.wait_ge(q["aux"][b], at(counted(c, 32)))
                dve.wait_ge(q["pM"], at((c + 1) * REL))
                dve.wait_ge(q["pR"], at(c))
                scan(run, 0, same[b][:, :], pb[:, 0:C], ALU.mult, ALU.add).then_inc(q["vA"], 1)
                dve.wait_ge(q["vA"], at(c + 1))
                step(carry(1))
                if there(c + 1):
                    masks(c + 1)

                def target_rows():
                    dve.wait_ge(q["pR"], at(c + 1))
                    dve.wait_ge(q["nD"], at(c))
                    step(V.tensor_tensor(yd[:, :, :], xd[b][:, :, :], flat_bank(pa), ALU.add))

                dense(dense_of(2, c)[0], target_rows, ((yd, 3),))

            def message_sums(c):
                b, q = c.parity(), ph[3]
                m, before = (run, run2) if b == 0 else (run2, run)
                dve.wait_ge(q["aux"][b], at(counted(c, 48)))
                dve.wait_ge(q["pR"], at(c + (-1)))
                for t in range(NT):
                    dve.wait_ge(q["eX"], at(c * NT + (t + 1)))
                    scan(m, t, same[b][:, :], masked[:, t, :], ALU.mult, ALU.add,
                         before[:, t, C:C + 1]).then_inc(q["vA"], 1)

            def layer3(c):
                b, q = c.parity(), ph[3]
                if there(c + 1):
                    message_sums(c + 1)
                for t in range(1, NT):
                    last = V.tensor_scalar(is_type[t - 1][0][:, :], ntd_all[:, c.v(), :], t, None, ALU.is_equal)
                step(last)
                dve.wait_ge(q["sel"], at(c + 1))
                settle(dve, s_passed)
                step(V.copy_predicated(ys[:, :, :], bc(is_type[0][0][:, :]), flat_bank(bank[6])))
                settle(dve, s_passed)
                step(V.copy_predicated(ys[:, :, :], bc(is_type[1][0][:, :]), flat_bank(bank[7])))
                dve.wait_ge(q["nD"], at(c))
                step(V.scalar_tensor_tensor(out=yd[:, :, :], in0=xd[b][:, :, :], scalar=2.0, in1=ys[:, :, :],
                                            op0=ALU.mult, op1=ALU.add))
                step(stats(yd, b, 3))
                rsqrt(b, 3, 4, (), q["vN"])

            over(dve, layer0, chain, DVE_STEPS[0])
            dve.wait_ge(s_rdeg, 16)
            V.reciprocal(degp[:, :], degp[:, :]).then_inc(s_rd, 1)
            step(V.memset(run[:, :, 0:1], 0.0))
            over(dve, layer1, chain, DVE_STEPS[1])
            step(V.memset(run[:, :, 0:1], 0.0))
            masks(Lin(0))
            over(dve, layer2, chain, DVE_STEPS[2])
            dense(Lin(NC))
            dense(Lin(NC + 1))
            step(V.memset(run2[:, :, C:C + 1], 0.0))
            message_sums(Lin(0))
            over(dve, layer3, chain, DVE_STEPS[3])

        @block.scalar
        def _(act):
            A = nc.scalar.activation

            def normalize(to, y, s, g):
                for j in range(T):
                    k = g * T + j
                    last = A(to[:, j, :], y[:, j, :], ACT.Identity, scale=rst[s][:, k:k + 1], bias=nmr[s][:, k:k + 1])
                return last

            def dense(d, edges=None):
                fixed = d.it is None
                first, second, third = (not fixed or 0 <= d.a - k < NC for k in range(3))
                s = d.parity()
                act.wait_ge(s_ln, at(d + 1))
                if second:
                    normalize(x3, y1, s, 1).then_inc(s_x3, 1)
                if first:
                    normalize(x1, y0[s], s, 2).then_inc(s_x1, 1)
                if second:
                    act.wait_ge(s_tr, at(d))
                    A(rt[:, :, :], by_tile(pt), ACT.Relu).then_inc(s_rt, 1)
                if third:
                    act.wait_ge(s_res[s], at((d + (-2)).half() * 16))
                    normalize(res[s], sel, s, 0).then_inc(s_out, 1)
                if first:
                    act.wait_ge(s_tx, at(d + 1))
                    A(xt[:, :, :], by_tile(pt), ACT.Copy).then_inc(s_xt, 1)
                if edges:
                    edges()
                if second:
                    act.wait_ge(s_o, at(d))
                    if third:
                        act.wait_ge(s_out, at(d + (-1)))
                    A(sel[:, :, :], flat_bank(po[0]), ACT.Copy).then_inc(s_sel, 1)

            natural = lambda a: a[:, :, :].rearrange("d p j -> d j p")

            def evacuate_sources(c, p, k):
                q = ph[p]
                act.wait_ge(q["tS"], at(c + 1))
                A(natural(st), by_tile(bank[k]), ACT.Copy).then_inc(q["eS"], 1)

            def evacuate_targets(c, p, k, to, func):
                q = ph[p]
                act.wait_ge(q["tD"], at(c + 1))
                A(natural(to), by_tile(bank[k]), func).then_inc(q["eD"], 1)

            def layer0(c):
                b, q = c.parity(), ph[0]
                d0, d1 = dense_of(0, c)
                act.wait_ge(q["vE"], at(c + 1))
                A(wb, wb, ACT.Exp)
                A(wa, wa, ACT.Exp).then_inc(q["eX"], 1)

                def source_rows():
                    act.wait_ge(q["stS"][b], at(c.half() * 16))
                    normalize(so[b], ysb[b], 0, 3).then_inc(q["nS"], 1)

                def target_rows():
                    act.wait_ge(q["stD"][b], at(c.half() * 16))
                    normalize(do[b], yd, 1, 3).then_inc(q["nD"], 1)

                dense(d0, source_rows)
                act.wait_ge(q["pR"], at(c + 1))
                act.wait_ge(s_ln, at(d0 + 1))
                A(den[:, 0:3 * H], pc[0:R, C:C + 3 * H], ACT.Copy)
                A(den[:, 3 * H:4 * H], pa[0:R, C:C + H], ACT.Copy).then_inc(q["eN"], 1)
                if there(c + 1):
                    evacuate_sources(c + 1, 0, 5)
                    evacuate_targets(c + 1, 0, 5, dt, ACT.Copy)
                dense(d1, target_rows)

            def layer1(c):
                b, q = c.parity(), ph[1]
                s = block_of(1, c).parity()
                if there(c + 1):
                    evacuate_sources(c + 1, 1, 7)
                    evacuate_targets(c + 1, 1, 7, dt, ACT.Copy)

                def edge_rows():
                    act.wait_ge(q["stS"][b], at(c.half() * 32))
                    normalize(so[b], ys, s, 3)
                    normalize(so3[b], ys, s, 4).then_inc(q["nS"], 1)
                    act.wait_ge(q["stD"][b], at(c.half() * 16))
                    normalize(do[b], yd, s, 5).then_inc(q["nD"], 1)

                dense(dense_of(1, c)[0], edge_rows)

            def layer2(c):
                b, q = c.parity(), ph[2]
                s = block_of(2, c).parity()
                if there(c + 2):
                    act.wait_ge(q["vM"], at((c + 2) * REL))
                    evacuate_sources(c + 2, 2, 7)

                def target_rows():
                    act.wait_ge(q["stD"][b], at(c.half() * 16))
                    normalize(do[b], yd, s, 3).then_inc(q["nD"], 1)

                dense(dense_of(2, c)[0], target_rows)

            def messages(c):
                b, q = c.parity(), ph[3]
                evacuate_sources(c, 3, 0)
                for t in range(NT):
                    act.wait_ge(q["pM"], at(c * NT + (t + 1)))
                    act.wait_ge(q["vA"], at(c * NT))
                    A(masked[:, t, :], bank[2 + t][:, 0:C], ACT.Relu, bias=bet[:, t:t + 1]).then_inc(q["eX"], 1)
                act.wait_ge(q["pR"], at(c + (-1)))
                evacuate_targets(c, 3, 1, (dt, agg)[b], ACT.Relu)

            def layer3(c):
                b, q = c.parity(), ph[3]
                if there(c + 1):
                    messages(c + 1)
                act.wait_ge(q["pR"], at(c + 1))
                act.wait_ge(q["vN"], at(c))
                A(ys[:, :, :], flat_bank(bank[5]), ACT.Copy).then_inc(q["sel"], 1)
                act.wait_ge(q["vN"], at(c + 1))
                act.wait_ge(q["sc"][b], at(c.half() * (16 * T)))
                normalize(do[b], yd, b, 3).then_inc(q["nD"], 1)

            act.wait_ge(s_w, 16 * NLOADS)
            evacuate_sources(Lin(0), 0, 5)
            evacuate_targets(Lin(0), 0, 5, dt, ACT.Copy)
            over(act, layer0)
            evacuate_sources(Lin(0), 1, 7)
            evacuate_targets(Lin(0), 1, 7, dt, ACT.Copy)
            over(act, layer1)
            evacuate_sources(Lin(0), 2, 7)
            act.wait_ge(ph[2]["vM"], REL)
            evacuate_sources(Lin(1), 2, 7)
            over(act, layer2)
            dense(Lin(NC))
            dense(Lin(NC + 1))
            messages(Lin(0))
            over(act, layer3)

        @block.tensor
        def _(pe):
            mm = nc.tensor.matmul

            def turn(to, rows_):
                for j in range(T):
                    last = nc.tensor.transpose(tile_of(to, j), rows_[:, j, :], ident[0:R, 0:R])
                return last

            def biased(to, i):
                mm(to[0:R, 0:T * D], ones_bf[:, 0:R], bparts[:, i, :, :].rearrange("k j d -> k (j d)"), start=True, stop=False, skip_group_check=True)

            def product(to, left, right, stop=True):
                for j in range(T):
                    last = mm(to[0:R, j * D:(j + 1) * D], left(j), right, start=False, stop=stop and j == T - 1, skip_group_check=True)
                return last

            pe.wait_ge(s_w, 16 * NLOADS)
            pe.wait_ge(s_bp, 1)
            for k in range(2):
                mm(bank[0][:, 0:D], b1m[:, k, :], w2[:, k, :], start=k == 0, stop=k == 1)
            for a in range(2):
                for k in range(2):
                    last = mm(bank[1][:, a * D:(a + 1) * D], w1t[:, k, a * D:(a + 1) * D], w2[:, k, :], start=k == 0, stop=k == 1)
            last.then_inc(s_pe0, 1)
            pe.wait_ge(s_bp, 2)
            pe.wait_ge(s_pchain, 1)

            pe.wait_ge(s_hs, 1)

            def dense_turns(d):
                fixed = d.it is None
                first, second = (not fixed or 0 <= d.a - k < NC for k in range(2))
                if second:
                    pe.wait_ge(s_x3, at(d))
                    pe.wait_ge(s_xt, at(d))
                    turn(pt, x3).then_inc(s_tr, 1)
                if first:
                    pe.wait_ge(s_x1, at(d + 1))
                    pe.wait_ge(s_rt, at(d))
                    turn(pt, x1).then_inc(s_tx, 1)

            def dense_products(d):
                fixed = d.it is None
                first, second = (not fixed or 0 <= d.a - k < NC for k in range(2))
                if second:
                    pe.wait_ge(s_rt, at(d))
                    pe.wait_ge(s_ln, at(d + 1))
                    for t in range(NT):
                        biased(po[t], 2 + t)
                        last = product(po[t], lambda j: rt[:, j, :], wnt[:, 0, t, :])
                    last.then_inc(s_o, 1)
                if first:
                    pe.wait_ge(s_xt, at(d + 1))
                    biased(pz, 0)
                    product(pz, lambda j: xt[:, j, :], wab[:, 0, :]).then_inc(s_z, 1)

            def front0(c):
                b, q = c.parity(), ph[0]
                pe.wait_ge(q["g"][b], at(counted(c, 32 * T)))
                pe.wait_ge(q["vA"], at(c))
                pe.wait_ge(q["eN"], at(c))
                turn(pa, xs[b]).then_inc(q["tS"], 1)
                pe.wait_ge(q["eS"], at(c + 1))
                turn(pa, xd[b]).then_inc(q["tD"], 1)
                pe.wait_ge(q["aux"][b], at(counted(c, 64)))
                pe.wait_ge(q["vE"], at(c))
                mm(pc[:, 0:C], ks[:, :], stf, start=True, stop=False)
                mm(pc[:, 0:C], es[:, :], ea[b][:, :], start=False, stop=False)
                pe.wait_ge(q["eD"], at(c + 1))
                mm(pc[:, 0:C], qs[:, :], dtf, start=False, stop=True).then_inc(q["pA"], 1)
                mm(pa[:, 0:C], wv[:, :], stf, start=True, stop=True).then_inc(q["pB"], 1)

            def layer0(c):
                b, q = c.parity(), ph[0]
                d0, d1 = dense_of(0, c)
                dense_turns(d0)
                dense_products(d0)
                pe.wait_ge(q["vA"], at(c + 1))
                for j in range(T):
                    mm(pb[0:R, j * D:(j + 1) * D], run_tile(run, 1, j), ident[:, :], start=True, stop=True)
                for j in range(T):
                    to = pc[0:R, C + j * H:C + (j + 1) * H] if j < T - 1 else pa[0:R, C:C + H]
                    last = mm(to, run_tile(run, 2, j), headsel[:, :], start=True, stop=True)
                last.then_inc(q["pR"], 1)
                if there(c + 1):
                    front0(c + 1)
                dense_turns(d1)
                dense_products(d1)

            def turns1(c):
                b, q = c.parity(), ph[1]
                pe.wait_ge(q["g"][b], at(counted(c, 16 * T)))
                pe.wait_ge(q["aux"][b], at(counted(c, 48)))
                turn(pc, xs[b]).then_inc(q["tS"], 1)
                pe.wait_ge(q["eS"], at(c + 1))
                turn(pc, xd[b]).then_inc(q["tD"], 1)

            def products1(c):
                q = ph[1]
                pe.wait_ge(q["eS"], at(c + 1))
                biased(pa, 0)
                product(pa, lambda j: st[:, :, j], wab[:, 0, :])
                pe.wait_ge(q["eD"], at(c + 1))
                biased(pb, 0)
                product(pb, lambda j: dt[:, :, j], wab[:, 0, :], stop=False)

            def layer1(c):
                q = ph[1]
                pe.wait_ge(q["vA"], at(c + 1))
                product(pb, lambda j: agg[:, :, j], wab[:, 1, :]).then_inc(q["pR"], 1)
                if there(c + 1):
                    turns1(c + 1)
                d = dense_of(1, c)[0]
                dense_turns(d)
                dense_products(d)
                if there(c + 1):
                    products1(c + 1)

            def turns2(c):
                b, q = c.parity(), ph[2]
                pe.wait_ge(q["g"][b], at(counted(c, 16 * T)))
                pe.wait_ge(q["eS"], at(c))
                turn(pc, xs[b]).then_inc(q["tS"], 1)

            def relations2(c):
                q = ph[2]
                pe.wait_ge(q["vA"], at(c))
                for r in range(REL):
                    pe.wait_ge(q["vM"], at(c * REL + (r + 1)))
                    mm(pb[:, 0:C], wr[:, r, :], masked[:, r, :], start=r == 0, stop=r == REL - 1).then_inc(q["pM"], 1)

            def layer2(c):
                q = ph[2]
                pe.wait_ge(q["vA"], at(c + 1))
                if c.it is not None or c.a >= 1:
                    pe.wait_ge(s_ln, at(block_of(2, c)))
                for j in range(T):
                    last = mm(pa[0:R, j * D:(j + 1) * D], run_tile(run, 0, j), ident[:, :], start=True, stop=True)
                last.then_inc(q["pR"], 1)
                if there(c + 1):
                    relations2(c + 1)
                if there(c + 2):
                    turns2(c + 2)
                d = dense_of(2, c)[0]
                dense_turns(d)
                dense_products(d)

            def messages(c):
                b, q = c.parity(), ph[3]
                pe.wait_ge(q["g"][b], at(counted(c, 16 * T)))
                pe.wait_ge(q["ld"][b], at(counted(c, 32)))
                pe.wait_ge(q["eS"], at(c))
                turn(bank[0], xs[b]).then_inc(q["tS"], 1)
                pe.wait_ge(q["eS"], at(c + 1))
                pe.wait_ge(q["eX"], at(c * NT))
                for t in range(NT):
                    mm(bank[2 + t][:, 0:C], ones_bf[0:1, :], off[b][0:1, t, :], start=True, stop=False)
                    mm(bank[2 + t][:, 0:C], wet[:, t, :], stf, start=False, stop=True).then_inc(q["pM"], 1)
                pe.wait_ge(q["aux"][b], at(counted(c, 48)))
                pe.wait_ge(q["eD"], at(c))
                turn(bank[1], xd[b]).then_inc(q["tD"], 1)

            def layer3(c):
                b, q = c.parity(), ph[3]
                if there(c + 1):
                    messages(c + 1)
                pe.wait_ge(q["eD"], at(c + 1))
                pe.wait_ge(q["vN"], at(c))
                own, sums = (dt, agg)[b], (run, run2)[b]
                for t in range(NT):
                    biased(bank[5 + t], 2 + t)
                    product(bank[5 + t], lambda j: own[:, :, j], wnt[:, 0, t, :], stop=False)
                for k in range(NT):
                    pe.wait_ge(q["vA"], at(c * NT + (k + 1)))
                    for t in range(NT):
                        last = product(bank[5 + t], lambda j: run_tile(sums, k, j), wnt[:, 1 + k, t, :], stop=k == NT - 1)
                last.then_inc(q["pR"], 1)

            front0(Lin(0))
            over(pe, layer0)
            turns1(Lin(0))
            products1(Lin(0))
            over(pe, layer1)
            turns2(Lin(0))
            relations2(Lin(0))
            turns2(Lin(1))
            over(pe, layer2)
            for d in (NC, NC + 1):
                dense_turns(Lin(d))
                dense_products(Lin(d))
            messages(Lin(0))
            over(pe, layer3)


def kernel(**inputs):
    import numpy as np
    import concourse.bacc as bacc
    from concourse.bass_utils import run_bass_kernel_spmd

    a = {k: np.asarray(v) for k, v in inputs.items()}
    W1, W2 = a["L1_gnn_W1"], a["L1_gnn_W2"]
    n, t = a["x"].shape[0], a["L3_gnn_W_e"].shape[0]
    laid = {
        "x": a["x"], "src": a["src"], "dst": a["dst"], "eattrT": a["edge_attr_64"].T,
        "etype3": a["edge_type_3"], "etype8": a["edge_type_8"][None], "eweight": a["edge_weight"][None],
        "ntype3": a["node_type_3"][:, None], "Wq": a["L0_gnn_Wq"], "Wk": a["L0_gnn_Wk"], "Wv": a["L0_gnn_Wv"],
        "We": a["L0_gnn_We"], "gate": a["L0_gnn_gate"], "bias0": a["L0_gnn_bias"][None],
        "W1T": W1.T.reshape(2, D, 2 * D).transpose(1, 0, 2), "b1": a["L1_gnn_b1"].reshape(2, D).T,
        "W2": W2.reshape(2, D, D).transpose(1, 0, 2), "b2": a["L1_gnn_b2"][None],
        "Wr": a["L2_gnn_weight"].transpose(1, 0, 2), "WeT": a["L3_gnn_W_e"].transpose(2, 0, 1),
        "beT": a["L3_gnn_b_e"].T, "WnT": a["L3_gnn_W_n"].reshape(t, D, 1 + t, D).transpose(3, 2, 0, 1),
        "bn": a["L3_gnn_b_n"], "ident": np.eye(D, dtype=np.float32),
    }
    nc = bacc.Bacc("TRN2", target_bir_lowering=False, num_devices=1)
    arrays, args = {}, []
    for name, v in laid.items():
        v = np.ascontiguousarray(v)
        arrays[f"in_{name}"] = v
        args.append(nc.dram_tensor(f"in_{name}", v.shape, mybir.dt.from_np(v.dtype), kind="ExternalInput").ap())
    args.append(nc.dram_tensor("out_rows", [n, D], F32, kind="ExternalOutput").ap())
    gnn_kernel(nc, *args)
    r = run_bass_kernel_spmd(nc, [arrays], core_ids=[0])
    return r.results[0]["out_rows"]
```

```python
from contextlib import ExitStack

import concourse.bass as bass
from concourse import mybir

F32 = mybir.dt.float32
BF16 = mybir.dt.bfloat16
I32 = mybir.dt.int32
ALU = mybir.AluOpType
ACT = mybir.ActivationFunctionType
AX_X = mybir.AxisListType.X

D = 128
R = 125
T = 4
C = R * T
EPS = 1e-5
TINY = 1e-16
BIG = 1e30
SKIP = 1 << 20
RSQRT_GUESS = 1597463007.0


class Lin:

    def __init__(self, a, s=0, it=None):
        self.a, self.s, self.it = a, s, it

    def __add__(self, n):
        return Lin(self.a + n, self.s, self.it)

    def __mul__(self, n):
        return Lin(self.a * n, self.s * n, self.it)

    def half(self):
        assert self.s % 2 == 0
        return Lin(self.a // 2, self.s // 2, self.it)

    def parity(self):
        return self.a % 2

    def v(self):
        return self.a if self.it is None or self.s == 0 else self.it * self.s + self.a


def at(count):
    if not isinstance(count, Lin):
        return max(count, 0)
    if count.it is None or count.s == 0:
        return max(count.a, 0)
    assert count.a > 0
    return count.v()


def settle(eng, sem):
    eng.sem_inc(sem, 1)


class Chain:

    def __init__(self, eng, sem):
        self.eng, self.sem, self.base, self.k, self.it, self.per = eng, sem, 0, 0, None, 0

    def step(self, ins):
        ins.then_inc(self.sem, 1)
        self.k += 1
        self.eng.wait_ge(self.sem, at(Lin(self.base + self.k, self.per, self.it)))

    def loop(self, it, per):
        self.base, self.k, self.it, self.per = self.base + self.k, 0, it, per

    def end(self, trips):
        assert self.k == self.per, f"{self.k} steps in the loop's body, {self.per} stated"
        self.base, self.k, self.it, self.per = self.base + trips * self.per, 0, None, 0


def gnn_kernel(nc, x, src, dst, eattrT, etype3, etype8, eweight, ntype3, Wq, Wk, Wv, We, gate,
               bias0, W1T, b1, W2, b2, Wr, WeT, beT, WnT, bn, ident_d, out):
    N, E = x.shape[0], src.shape[0]
    NC, EC = N // C, E // C
    PEEL, TAIL = 3, 4
    TR = (EC - PEEL - TAIL) // 2
    H = gate.shape[0]
    HC = D // H
    ED = eattrT.shape[0]
    REL = Wr.shape[1]
    NT = WeT.shape[1]
    INV = float(HC) ** -0.5
    PM = E // R
    assert N % C == 0 and E % C == 0 and (EC - PEEL - TAIL) % 2 == 0 and NC == 4 * EC

    rows = lambda a: a.rearrange("(n p j) d -> n p (j d)", p=R, j=T)
    x_c, out_c = rows(x), rows(out)
    src_c = src.rearrange("(n p j) -> n p j", p=R, j=T)
    dst_c = dst.rearrange("(n p j) -> n p j", p=R, j=T)
    nt_c = ntype3.rearrange("(n p j) o -> n p (j o)", p=R, j=T)

    s_rows = [nc.dram_tensor(f"source_rows{i}", [E, D], F32).ap() for i in (1, 2, 3)]
    d_rows = [nc.dram_tensor(f"target_rows{i}", [E, D], F32).ap() for i in (1, 2, 3)]
    same_d = nc.dram_tensor("same_d", [1, E], F32).ap()
    start_d = nc.dram_tensor("start_d", [1, E], F32).ap()
    deg_d = nc.dram_tensor("deg_d", [1, E], F32).ap()
    rdeg_d = nc.dram_tensor("rdeg_d", [1, E], F32).ap()
    last_d = nc.dram_tensor("last_d", [E], I32).ap()
    off_d = nc.dram_tensor("off_d", [NT, E], BF16).ap()
    slot_d = nc.dram_tensor("slot_d", [N, 1], I32).ap()
    last_c = last_d.rearrange("(n p j) -> n p j", p=R, j=T)

    ctx = ExitStack()
    with ctx:
        def sb(name, shape, dt=F32):
            return ctx.enter_context(nc.sbuf_tensor(name, shape, dt))

        def sem(name):
            return ctx.enter_context(nc.semaphore(name))

        def two(make, name, *a):
            return [make(f"{name}{i}", *a) for i in range(2)]

        wq, wk, wv = sb("wq", [D, D]), sb("wk", [D, D]), sb("wv", [D, D])
        qs, ks = sb("qs", [D, D]), sb("ks", [D, D])
        we, es = sb("we", [ED, D]), sb("es", [ED + 1, D])
        head = sb("head", [D, 3, H])
        gate_sb = sb("gate_sb", [ED + 1, H])
        w1t, w2 = sb("w1t", [D, 2, 2 * D]), sb("w2", [D, 2, D])
        b1c, b1m = sb("b1c", [D, 2]), sb("b1m", [D, 2, D])
        wab = sb("wab", [D, 2, D])
        wr, wet, wnt = sb("wr", [D, REL, D]), sb("wet", [D, NT, D]), sb("wnt", [D, 1 + NT, NT, D])
        bet = sb("bet", [D, NT])
        ident = sb("ident", [D, D])
        bias_bc = sb("bias_bc", [R, D])
        brow = sb("brow", [D, 2 + NT, D])
        b2row = sb("b2row", [D, D])
        brest = sb("brest", [D, 2 + NT, D])
        bhi, bmid, blo = (sb(n, [D, 2 + NT, D], BF16) for n in ("bhi", "bmid", "blo"))
        bparts = sb("bparts", [D, 2 + NT, T, D], BF16)
        ones_f = sb("ones_f", [D, 1])
        ones_bf = sb("ones_bf", [D, D], BF16)
        cur, prv, nxt = (sb(n, [R, PM], I32) for n in ("cur", "prv", "nxt"))
        ty = sb("ty", [R, PM], I32)
        same_p, start_p, more_p = (sb(n, [R, PM]) for n in ("same_p", "start_p", "more_p"))
        last_p = sb("last_p", [R, PM], I32)
        off_p = sb("off_p", [R, NT, PM], BF16)
        fill = sb("fill", [R, N // R], I32)
        eid = sb("eid", [R, EC, T], I32)
        slot_all, ntd_all = sb("slot_all", [R, EC, T], I32), sb("ntd_all", [R, EC, T], I32)
        xin, ntin = two(sb, "xin", [R, T, D]), two(sb, "ntin", [R, T], I32)
        y0 = two(sb, "y0_", [R, T, D])
        y1, sel = sb("y1", [R, T, D]), two(sb, "sel", [R, T, D])
        x1, x3 = two(sb, "x1_", [R, T, D]), two(sb, "x3_", [R, T, D])
        xt = sb("xt", [D, T, R])
        rt = sb("rt", [D, T, R])
        res = two(sb, "res", [R, T, D])
        is_type = [two(sb, f"is_type{t}_", [R, T], I32) for t in range(1, NT)]
        G = 6
        bst = two(sb, "bst", [R, G * T, 6])
        msum, mdif, ve, rst, nmr, tmp = (two(sb, n, [R, G * T]) for n in
                                             ("msum", "mdif", "ve", "rst", "nmr", "tmp"))
        xs, xd = two(sb, "xs", [R, T, D]), two(sb, "xd", [R, T, D])
        isrc, idst, ilast, ieid = (two(sb, n, [R, T], I32) for n in ("isrc", "idst", "ilast", "ieid"))
        islot, intd = two(sb, "islot", [R, T], I32), two(sb, "intd", [R, T], I32)
        st, dt = sb("st", [D, R, T]), sb("dt", [D, R, T])
        stf, dtf = (a[:, :, :].rearrange("d p j -> d (p j)") for a in (st, dt))
        ea = two(sb, "ea", [ED + 1, C])
        same = two(sb, "same", [D, C])
        aux = two(sb, "aux", [D, C])
        rel = two(sb, "rel", [D, C], I32)
        off = two(sb, "off", [1, NT, C], BF16)
        rows_same = two(sb, "rows_same", [1, C])
        deg = two(sb, "deg", [1, C])
        degp = sb("degp", [R, PM])
        run, run2 = sb("run", [D, 3, C + 1]), sb("run2", [D, 3, C + 1])
        masked = sb("masked", [D, REL, C])
        den = sb("den", [R, T * H])
        headsel = sb("headsel", [D, H])
        wa, wb, wc = (masked[:, k, :] for k in range(3))
        agg = sb("agg", [D, R, T])
        aggf = agg[:, :, :].rearrange("d p j -> d (p j)")
        ys, yd = sb("ys", [R, T, D]), sb("yd", [R, T, D])
        so, so3, do = (two(sb, n, [R, T, D]) for n in ("so", "so3", "do"))
        ysb, xdb = so3, two(sb, "xdb", [R, T, D])

        bank = [ctx.enter_context(nc.psum_tensor(f"bank{i}", [D, 512], F32)) for i in range(8)]
        pt, pz, po = bank[0], bank[1], bank[2:5]
        pa, pb, pc = bank[5:8]

        s_w, s_idx, s_slotrow, s_prep, s_scr, s_pe0, s_bp, s_const = map(
            sem, ("s_w", "s_idx", "s_slotrow", "s_prep", "s_scr", "s_pe0", "s_bp", "s_const"))
        s_fill, s_passed, s_rdeg, s_rd, s_hs = map(sem, ("s_fill", "s_passed", "s_rdeg", "s_rd", "s_hs"))
        s_xin, s_nt, s_res = two(sem, "s_xin"), two(sem, "s_nt"), two(sem, "s_res")
        s_read = sem("s_read")
        s_y0, s_ln, s_x1, s_x3, s_out = map(sem, ("s_y0", "s_ln", "s_x1", "s_x3", "s_out"))
        s_tx, s_xt, s_z, s_tr, s_rt, s_o, s_sel = map(sem, ("s_tx", "s_xt", "s_z", "s_tr", "s_rt", "s_o", "s_sel"))
        s_chain, s_pchain = sem("s_chain"), sem("s_pchain")

        SINGLE = ("tS tD eS eD pA pB pR vA vE eX nS nD yb eN", "tS tD eS eD pR vA nS nD rd",
                  "tS eS pM pR vA vM nD", "tS tD eS eD pM pR vA eX vN nD sel rd")
        PAIRS = ("aux idx g stS stD sc dg", "ld aux ix g gi stS stD", "ld aux rl ix g gi stD", "ld aux ix g sc")

        ph = [{**{k: sem(f"layer{n}_{k}") for k in SINGLE[n].split()},
               **{k: two(sem, f"layer{n}_{k}_") for k in PAIRS[n].split()}} for n in range(4)]

        def counted(chunk, per):
            return (chunk.half() + 1) * per

        def over(eng, body, chain=None, per=0):
            for c in range(PEEL):
                body(Lin(c))
            with eng.Fori(0, TR) as it:
                if chain:
                    chain.loop(it, per)
                body(Lin(PEEL, 2, it))
                body(Lin(PEEL + 1, 2, it))
            if chain:
                chain.end(TR)
            for c in range(EC - TAIL, EC):
                body(Lin(c))

        def there(c):
            return c.it is not None or c.a < EC

        def dense_of(p, c):
            if p == 0:
                return [c * 2, c * 2 + 1]
            return [c + (2 * EC if p == 1 else 3 * EC)] if p < 3 else []

        def block_of(p, c):
            return dense_of(p, c)[-1]

        NLOADS = 16 + NT
        DVE_STEPS = (82, 34, 34, 32)
        POOL_STEPS = (2, 2, 4, 2)
        one_row = ones_f[0:1, 0:1].broadcast_to([1, C])
        run_tile = lambda m, k, j: m[:, k, 1:C + 1].rearrange("d (p j) -> d p j", j=T)[:, :, j]
        block = ctx.enter_context(nc.Block())

        @block.sync
        def _(sp):
            pm = lambda a: a.rearrange("(p t) -> p t", t=PM)
            sp.wait_ge(s_const, 1)
            sp.dma_start(cur[:, :], pm(dst)).then_inc(s_idx, 16)
            sp.dma_start(prv[1:R, :], bass.AP(dst.tensor, PM - 1, [[PM, R - 1], [1, PM]])).then_inc(s_idx, 16)
            sp.dma_start(prv[0:1, 1:PM], bass.AP(dst.tensor, 0, [[PM, 1], [1, PM - 1]])).then_inc(s_idx, 16)
            sp.dma_start(nxt[0:R - 1, :], bass.AP(dst.tensor, 1, [[PM, R - 1], [1, PM]])).then_inc(s_idx, 16)
            sp.dma_start(nxt[R - 1:R, 0:PM - 1], bass.AP(dst.tensor, E - PM + 1, [[PM, 1], [1, PM - 1]])).then_inc(s_idx, 16)
            sp.dma_start(ty[:, :], pm(etype3)).then_inc(s_idx, 16)
            loads = [(ident[:, :], ident_d), (bias_bc[:, :], bias0[0:1, :].broadcast_to([R, D])),
                     (wq[:, :], Wq), (wk[:, :], Wk), (wv[:, :], Wv), (we[:, :], We),
                     (gate_sb[ED:ED + 1, :], gate[None, :]), (w1t[:, :, :], W1T), (w2[:, :, :], W2),
                     (b1c[:, :], b1), (b2row[:, :], b2[0:1, :].broadcast_to([D, D])),
                     (brow[:, 1, :], bias0[0:1, :].broadcast_to([D, D])),
                     (wr[:, :, :], Wr), (wet[:, :, :], WeT), (wnt[:, :, :, :], WnT), (bet[:, :], beT)]
            loads += [(brow[:, 2 + t, :], bn[t:t + 1, :].broadcast_to([D, D])) for t in range(NT)]
            for to, of in loads:
                sp.dma_start(to, of).then_inc(s_w, 16)
            sp.wait_ge(s_prep, 1)
            sp.wait_ge(s_fill, 1)
            row = lambda a: a.rearrange("o (p t) -> (o p) t", t=PM)
            sp.dma_start(slot_d.rearrange("(p t) o -> p (t o)", p=R), fill[:, :]).then_inc(s_slotrow, 16)
            sp.dma_start(row(same_d), same_p[:, :]).then_inc(s_scr, 16)
            sp.dma_start(row(start_d), start_p[:, :]).then_inc(s_scr, 16)
            sp.dma_start(pm(last_d), last_p[:, :]).then_inc(s_scr, 16)
            for t in range(NT):
                sp.dma_start(off_d[t].rearrange("(p t) -> p t", t=PM), off_p[:, t, :]).then_inc(s_scr, 16)
            sp.wait_ge(s_scr, 16 * (3 + NT))

            flat = lambda a: a[:, :, :].rearrange("p j d -> p (j d)")
            cols = lambda c: bass.ds(c.v() * C, C)
            to_all = lambda a, c: a[0:1, cols(c)].broadcast_to([D, C])

            def load_dense(d):
                b = d.parity()
                if d.it is not None or d.a < NC:
                    sp.wait_ge(s_y0, at(d + (-1)))
                    sp.dma_start(flat(xin[b]), x_c[d.v()]).then_inc(s_xin[b], 16)
                if d.it is not None or d.a >= 4:
                    sp.wait_ge(s_read, at(d + (-1)))
                    sp.dma_start(ntin[b][:, :], nt_c[(d + (-4)).v()]).then_inc(s_nt[b], 16)

            def store_dense(d):
                b = d.parity()
                sp.wait_ge(s_out, at(d + 1))
                sp.dma_start(out_c[d.v()], flat(res[b])).then_inc(s_res[b], 16)

            def indices0(c):
                b, q = c.parity(), ph[0]
                sp.wait_ge(q["g"][b], at(c.half() * (32 * T)))
                settle(sp, s_passed)
                sp.wait_ge(q["sc"][b], at(c.half() * (16 * T)))
                sp.dma_start(isrc[b][:, :], src_c[c.v()]).then_inc(q["idx"][b], 16)
                sp.dma_start(idst[b][:, :], dst_c[c.v()]).then_inc(q["idx"][b], 16)
                sp.dma_start(ilast[b][:, :], last_c[c.v()]).then_inc(q["idx"][b], 16)

            def features0(c):
                b, q = c.parity(), ph[0]
                sp.wait_ge(q["vA"], at(c + (-1)))
                sp.dma_start(ea[b][0:ED, :], eattrT[:, cols(c)]).then_inc(q["aux"][b], 16)
                sp.dma_start(ea[b][ED:ED + 1, :], eweight[0:1, cols(c)]).then_inc(q["aux"][b], 16)
                sp.dma_start(rows_same[b][:, :], same_d[0:1, cols(c)]).then_inc(q["aux"][b], 16)
                sp.dma_start(aux[b][:, :], to_all(start_d, c)).then_inc(q["aux"][b], 16)

            def store0(c):
                b, q = c.parity(), ph[0]
                sp.wait_ge(q["vA"], at(c + 1))
                sp.dma_start(deg_d[0:1, cols(c)], deg[b][:, :]).then_inc(q["dg"][b], 16)
                sp.wait_ge(q["nS"], at(c + 1))
                sp.dma_start(rows(s_rows[0])[c.v()], flat(so[b])).then_inc(q["stS"][b], 16)
                sp.wait_ge(q["nD"], at(c + 1))
                sp.dma_start(rows(d_rows[0])[c.v()], flat(do[b])).then_inc(q["stD"][b], 16)

            def indices1(c):
                b, q = c.parity(), ph[1]
                sp.wait_ge(q["gi"][b], at(c.half() * (16 * T)))
                sp.dma_start(isrc[b][:, :], src_c[c.v()]).then_inc(q["ix"][b], 16)

            def rows1(c):
                b, q = c.parity(), ph[1]
                if c.it is not None or c.a >= 2:
                    sp.wait_ge(s_ln, at(block_of(1, c) + (-1)))
                sp.dma_start(flat(xs[b]), rows(s_rows[0])[c.v()]).then_inc(q["ld"][b], 16)
                sp.dma_start(flat(xd[b]), rows(d_rows[0])[c.v()]).then_inc(q["aux"][b], 16)
                sp.dma_start(same[b][:, :], to_all(same_d, c)).then_inc(q["aux"][b], 16)
                sp.dma_start(aux[b][:, :], to_all(rdeg_d, c)).then_inc(q["aux"][b], 16)

            def store1(c):
                b, q = c.parity(), ph[1]
                sp.wait_ge(q["nS"], at(c + 1))
                sp.dma_start(rows(s_rows[1])[c.v()], flat(so[b])).then_inc(q["stS"][b], 16)
                sp.dma_start(rows(s_rows[2])[c.v()], flat(so3[b])).then_inc(q["stS"][b], 16)
                sp.wait_ge(q["nD"], at(c + 1))
                sp.dma_start(rows(d_rows[1])[c.v()], flat(do[b])).then_inc(q["stD"][b], 16)

            def indices2(c):
                b, q = c.parity(), ph[2]
                sp.wait_ge(q["gi"][b], at(c.half() * (16 * T)))
                sp.dma_start(idst[b][:, :], dst_c[c.v()]).then_inc(q["ix"][b], 16)

            def sources2(c):
                b, q = c.parity(), ph[2]
                sp.wait_ge(q["tS"], at(c + (-1)))
                sp.dma_start(flat(xs[b]), rows(s_rows[1])[c.v()]).then_inc(q["ld"][b], 16)

            def relations2(c):
                b, q = c.parity(), ph[2]
                sp.wait_ge(q["vM"], at((c + (-1)) * REL))
                sp.dma_start(rel[b][:, :], to_all(etype8, c)).then_inc(q["rl"][b], 16)

            def targets2(c):
                b, q = c.parity(), ph[2]
                if c.it is not None or c.a >= 2:
                    sp.wait_ge(s_ln, at(block_of(2, c) + (-1)))
                sp.dma_start(flat(xd[b]), rows(d_rows[1])[c.v()]).then_inc(q["aux"][b], 16)
                sp.dma_start(same[b][:, :], to_all(same_d, c)).then_inc(q["aux"][b], 16)

            def store2(c):
                b, q = c.parity(), ph[2]
                sp.wait_ge(q["nD"], at(c + 1))
                sp.dma_start(rows(d_rows[2])[c.v()], flat(do[b])).then_inc(q["stD"][b], 16)

            def sources3(c):
                b, q = c.parity(), ph[3]
                sp.wait_ge(q["tS"], at(c + (-1)))
                settle(sp, s_passed)
                sp.wait_ge(q["pM"], at((c + (-1)) * NT))
                sp.dma_start(flat(xs[b]), rows(s_rows[2])[c.v()]).then_inc(q["ld"][b], 16)
                sp.dma_start(off[b][:, :, :], off_d[:, cols(c)][None]).then_inc(q["ld"][b], 16)

            def targets3(c):
                b, q = c.parity(), ph[3]
                sp.wait_ge(q["rd"], at(c + (-1)))
                sp.dma_start(flat(xd[b]), rows(d_rows[2])[c.v()]).then_inc(q["aux"][b], 16)
                sp.dma_start(same[b][:, :], to_all(same_d, c)).then_inc(q["aux"][b], 16)

            def places3(c):
                b, q = c.parity(), ph[3]
                sp.wait_ge(q["sc"][b], at(c.half() * (16 * T)))
                sp.dma_start(ilast[b][:, :], last_c[c.v()]).then_inc(q["ix"][b], 16)

            def stored(p):
                for b in range(2):
                    n = (EC + 1 - b) // 2
                    if p < 2:
                        sp.wait_ge(ph[p]["stS"][b], (1 + p) * 16 * n)
                    if p == 0:
                        sp.wait_ge(ph[p]["dg"][b], 16 * n)
                    sp.wait_ge(ph[p]["stD"][b], 16 * n)

            plan = (((indices0, 2), (features0, 2)), ((indices1, 3), (rows1, 1)),
                    ((sources2, 3), (indices2, 1), (relations2, 2), (targets2, 1)), ((sources3, 2), (targets3, 1), (places3, 0)))
            stores = (store0, store1, store2, None)
            at_once = (indices0, indices1, rows1, sources2, indices2, relations2, targets2, sources3)
            load_dense(Lin(0))
            for p in range(4):
                if p:
                    stored(p - 1)
                if p == 1:
                    sp.dma_start(degp[:, :], deg_d.rearrange("o (p t) -> (o p) t", t=PM)).then_inc(s_rdeg, 16)
                    sp.wait_ge(s_rd, 1)
                    sp.dma_start(rdeg_d.rearrange("o (p t) -> (o p) t", t=PM), degp[:, :]).then_inc(s_rdeg, 16)
                    sp.wait_ge(s_rdeg, 32)
                for load, ahead in plan[p]:
                    for c in range(ahead):
                        load(Lin(c))

                def loads_of(c, early):
                    for load, ahead in plan[p]:
                        if there(c + ahead) and (load in at_once) == early:
                            load(c + ahead)

                def body(c):
                    loads_of(c, True)
                    for i, d in enumerate(dense_of(p, c)):
                        load_dense(d + 1)
                        if d.it is not None or d.a >= 5:
                            store_dense(d + (-5))
                        if i == 0 and stores[p] and (c.it is not None or c.a >= 1):
                            stores[p](c + (-1))
                    loads_of(c, False)

                over(sp, body)
                if stores[p]:
                    stores[p](Lin(EC - 1))
                if p == 2:
                    for d in range(NC, NC + 4):
                        if d < NC + 3:
                            load_dense(Lin(d + 1))
                        store_dense(Lin(d - 5))
                    store_dense(Lin(NC - 1))

        bc = lambda a: a.unsqueeze(2).broadcast_to([R, T, D])
        tile_of = lambda a, j: a[:, j * R:(j + 1) * R]
        flat_bank = lambda k: k[0:R, 0:T * D].rearrange("p (j d) -> p j d", j=T)
        by_tile = lambda k: k[:, 0:C].rearrange("d (j p) -> d j p", j=T)
        bias_rows = bias_bc[:, :].unsqueeze(1).broadcast_to([R, T, D])

        @block.gpsimd
        def _(pool):
            chain = Chain(pool, s_pchain)
            nc.gpsimd.memset(prv[:, :], -1)
            nc.gpsimd.memset(nxt[:, :], -1).then_inc(s_const, 1)
            nc.gpsimd.memset(fill[:, :], SKIP).then_inc(s_fill, 1)
            nc.gpsimd.iota(eid[:, :, :], pattern=[[C, EC], [1, T]], base=0, channel_multiplier=T)
            nc.gpsimd.memset(ones_f[:, :], 1.0)
            chain.step(nc.gpsimd.memset(ones_bf[:, :], 1.0))

            def gather(to, table, index, j, bound):
                if j == 0:
                    settle(pool, s_passed)
                return nc.gpsimd.indirect_dma_start(
                    out=to, out_offset=None, in_=table,
                    in_offset=bass.IndirectOffsetOnAxis(ap=index[:, j:j + 1], axis=0),
                    bounds_check=bound, oob_is_err=False)

            def scatter(table, index, j, of):
                if j == 0:
                    settle(pool, s_passed)
                return nc.gpsimd.indirect_dma_start(
                    out=table, out_offset=bass.IndirectOffsetOnAxis(ap=index[:, j:j + 1], axis=0),
                    in_=of, in_offset=None, bounds_check=N - 1, oob_is_err=False)

            def add_bias(d):
                b = d.parity()
                pool.wait_ge(s_xin[b], at(counted(d, 16)))
                pool.wait_ge(s_x1, at(d + (-1)))
                nc.gpsimd.tensor_tensor(y0[b][:, :, :], xin[b][:, :, :], bias_rows, ALU.add).then_inc(s_y0, 1)

            def rows0(c):
                b, q = c.parity(), ph[0]
                pool.wait_ge(q["idx"][b], at(counted(c, 48)))
                pool.wait_ge(q["tD"], at(c + (-1)))
                for j in range(T):
                    gather(xs[b][:, j, :], x, isrc[b], j, N - 1).then_inc(q["g"][b], 16)
                    gather(xd[b][:, j, :], x, idst[b], j, N - 1).then_inc(q["g"][b], 16)

            def marks0(c):
                b, q = c.parity(), ph[0]
                chain.step(nc.gpsimd.tensor_copy(ieid[b][:, :], eid[:, c.v(), :]))
                if c.it is None and c.a == 0:
                    pool.wait_ge(s_slotrow, 16)
                for j in range(T):
                    scatter(slot_d, ilast[b], j, ieid[b][:, j:j + 1]).then_inc(q["sc"][b], 16)
                pool.wait_ge(q["g"][b], at(counted(c, 32 * T)))
                pool.wait_ge(q["nD"], at(c + (-1)))
                nc.gpsimd.tensor_tensor(ysb[b][:, :, :], xs[b][:, :, :], bias_rows, ALU.add)
                nc.gpsimd.tensor_tensor(xdb[b][:, :, :], xd[b][:, :, :], bias_rows, ALU.add).then_inc(q["yb"], 1)

            def layer0(c):
                d0, d1 = dense_of(0, c)
                add_bias(d0)
                if there(c + 1):
                    rows0(c + 1)
                add_bias(d1)
                if there(c + 1):
                    marks0(c + 1)

            def slots1(c):
                b, q = c.parity(), ph[1]
                pool.wait_ge(q["ix"][b], at(counted(c, 16)))
                pool.wait_ge(q["g"][b], at(c.half() * (16 * T)))
                for j in range(T):
                    gather(islot[b][:, j:j + 1], slot_d, isrc[b], j, N - 1).then_inc(q["gi"][b], 16)

            def rows1(c):
                b, q = c.parity(), ph[1]
                pool.wait_ge(q["gi"][b], at(counted(c, 16 * T)))
                pool.wait_ge(q["ld"][b], at(counted(c, 16)))
                for j in range(T):
                    gather(xs[b][:, j, :], d_rows[0], islot[b], j, E - 1).then_inc(q["g"][b], 16)
                chain.step(nc.gpsimd.tensor_copy(slot_all[:, c.v(), :], islot[b][:, :]))
                settle(pool, s_passed)

            def layer1(c):
                add_bias(dense_of(1, c)[0])
                if there(c + 1):
                    rows1(c + 1)
                if there(c + 2):
                    slots1(c + 2)

            def updated(p, c):
                b, q = c.parity(), ph[p]
                pool.wait_ge(q["g"][b], at(c.half() * (16 * T)))
                settle(pool, s_passed)
                chain.step(nc.gpsimd.tensor_copy(islot[b][:, :], slot_all[:, c.v(), :]))
                pool.wait_ge(q["ld"][b], at(counted(c, 16 if p == 2 else 32)))
                for j in range(T):
                    gather(xs[b][:, j, :], d_rows[p - 1], islot[b], j, E - 1).then_inc(q["g"][b], 16)

            def types2(c):
                b, q = c.parity(), ph[2]
                pool.wait_ge(q["ix"][b], at(counted(c, 16)))
                for j in range(T):
                    gather(intd[b][:, j:j + 1], ntype3, idst[b], j, N - 1).then_inc(q["gi"][b], 16)
                pool.wait_ge(q["gi"][b], at(counted(c, 16 * T)))
                settle(pool, s_passed)
                chain.step(nc.gpsimd.tensor_copy(ntd_all[:, c.v(), :], intd[b][:, :]))
                settle(pool, s_passed)

            def layer2(c):
                add_bias(dense_of(2, c)[0])
                if there(c + 2):
                    updated(2, c + 2)
                types2(c)

            def layer3(c):
                b, q = c.parity(), ph[3]
                if there(c + 2):
                    updated(3, c + 2)
                if c.it is not None or c.a >= 1:
                    results3(c + (-1))

            def results3(c):
                b, q = c.parity(), ph[3]
                if c.it is None and c.a == 0:
                    for k in range(2):
                        pool.wait_ge(s_res[k], 16 * (NC // 2))
                pool.wait_ge(q["nD"], at(c + 1))
                pool.wait_ge(q["ix"][b], at(counted(c, 16)))
                for j in range(T):
                    scatter(out, ilast[b], j, do[b][:, j, :]).then_inc(q["sc"][b], 16)

            def landed(p):
                for b in range(2):
                    n = (EC + 1 - b) // 2
                    if p == 1:
                        pool.wait_ge(ph[0]["sc"][b], 16 * T * n)
                    pool.wait_ge(ph[p - 1]["stD"][b], 16 * n)
                    pool.wait_ge(ph[p - 1]["g"][b], (32 if p == 1 else 16) * T * n)

            rows0(Lin(0))
            marks0(Lin(0))
            over(pool, layer0, chain, POOL_STEPS[0])
            landed(1)
            slots1(Lin(0))
            rows1(Lin(0))
            slots1(Lin(1))
            over(pool, layer1, chain, POOL_STEPS[1])
            for p, layer in ((2, layer2), (3, layer3)):
                landed(p)
                updated(p, Lin(0))
                updated(p, Lin(1))
                over(pool, layer, chain, POOL_STEPS[p])
            results3(Lin(EC - 1))
            for b in range(2):
                pool.wait_ge(ph[3]["sc"][b], 16 * T * ((EC + 1 - b) // 2))

        @block.vector
        def _(dve):
            V = nc.vector
            chain = Chain(dve, s_chain)
            step = chain.step
            dve.wait_ge(s_idx, 96)
            V.tensor_tensor(same_p[:, :], cur[:, :], prv[:, :], ALU.is_equal)
            V.tensor_tensor(more_p[:, :], cur[:, :], nxt[:, :], ALU.is_equal)
            for t in range(NT):
                V.tensor_scalar(off_p[:, t, :], ty[:, :], t, -BIG, ALU.not_equal, ALU.mult)
            step(V.memset(run[:, :, :], 0.0))
            V.tensor_scalar(start_p[:, :], same_p[:, :], -1.0, BIG, ALU.add, ALU.mult)
            V.scalar_tensor_tensor(out=last_p[:, :], in0=more_p[:, :], scalar=float(SKIP), in1=cur[:, :],
                                   op0=ALU.mult, op1=ALU.add).then_inc(s_prep, 1)
            dve.wait_ge(s_w, 16 * NLOADS)
            for i, w in enumerate((wq, wk)):
                V.tensor_reduce(head[:, i, :], w[:, :].rearrange("k (h c) -> k h c", h=H), AX_X, ALU.add)
            V.tensor_reduce(head[0:ED, 2, :], we[:, :].rearrange("k (h c) -> k h c", h=H), AX_X, ALU.add)
            V.tensor_copy(b1m[:, :, :], b1c[:, :].unsqueeze(2).broadcast_to([D, 2, D]))
            step(V.memset(bparts[:, :, :, :], 0.0))
            heads = lambda a, n: a.unsqueeze(2).broadcast_to([n, H, HC])
            for i, w in enumerate((qs, ks)):
                V.tensor_scalar(w[:, :].rearrange("k (h c) -> k h c", h=H), heads(head[:, i, :], D), INV, None, ALU.mult)
            V.tensor_scalar(es[0:ED, :].rearrange("k (h c) -> k h c", h=H), heads(head[0:ED, 2, :], ED), INV, None, ALU.mult)
            V.tensor_copy(es[ED:ED + 1, :].rearrange("k (h c) -> k h c", h=H),
                          heads(gate_sb[ED:ED + 1, :], 1)).then_inc(s_bp, 1)
            dve.wait_ge(s_pe0, 1)
            V.tensor_copy(wab[:, :, :], bank[1][:, 0:2 * D].rearrange("k (a d) -> k a d", a=2))
            step(V.tensor_tensor(brow[:, 0, :], bank[0][:, 0:D], b2row[:, :], ALU.add))
            step(V.tensor_copy(bhi[:, :, :], brow[:, :, :]))
            step(V.tensor_tensor(brest[:, :, :], brow[:, :, :], bhi[:, :, :], ALU.subtract))
            step(V.tensor_copy(bmid[:, :, :], brest[:, :, :]))
            step(V.tensor_tensor(brest[:, :, :], brest[:, :, :], bmid[:, :, :], ALU.subtract))
            step(V.tensor_copy(blo[:, :, :], brest[:, :, :]))
            for part, p in ((bhi, 0), (bmid, 32), (blo, 64)):
                for j in range(T):
                    last = V.tensor_copy(bparts[p:p + 1, :, j, :], part[p:p + 1, :, :])
            last.then_inc(s_bp, 1)

            V.tensor_copy(headsel[:, :], ident[:, :].rearrange("k (h c) -> k h c", h=H)[:, :, 0]).then_inc(s_hs, 1)

            def stats(y, s, g):
                for j in range(T):
                    last = V.bn_stats(bst[s][:, g * T + j, :], y[:, j, :])
                return last

            def rsqrt(s, lo, hi, twice, done):
                g = slice(lo * T, hi * T)
                b_, ms, md, v, r, t, n = (a[s] for a in (bst, msum, mdif, ve, rst, tmp, nmr))
                ends = sorted({lo, hi} | {k + i for k in twice if lo <= k < hi for i in (0, 1)})
                parts = [(slice(i * T, j * T), i in twice) for i, j in zip(ends, ends[1:])]
                V.tensor_tensor(ms[:, g], b_[:, g, 1], b_[:, g, 4], ALU.add)
                V.tensor_tensor(md[:, g], b_[:, g, 1], b_[:, g, 4], ALU.subtract)
                step(V.tensor_tensor(v[:, g], b_[:, g, 2], b_[:, g, 5], ALU.add))
                for a, both in parts:
                    V.tensor_scalar(v[:, a], v[:, a], (1.0 + EPS if both else 1.0) / D, EPS * EPS if both else EPS, ALU.mult, ALU.add)
                step(V.tensor_tensor(md[:, g], md[:, g], md[:, g], ALU.mult))
                for a, both in parts:
                    last = V.scalar_tensor_tensor(out=v[:, a], in0=md[:, a], scalar=(1.0 + EPS if both else 1.0) / 4.0,
                                                  in1=v[:, a], op0=ALU.mult, op1=ALU.add)
                step(last)
                step(V.tensor_scalar(r[:, g].bitcast(I32), v[:, g].bitcast(I32), -0.5, RSQRT_GUESS, ALU.mult, ALU.add))
                for k in range(3):
                    step(V.scalar_tensor_tensor(out=t[:, g], in0=r[:, g], scalar=-0.5, in1=r[:, g], op0=ALU.mult, op1=ALU.mult))
                    step(V.tensor_tensor(t[:, g], t[:, g], v[:, g], ALU.mult))
                    if k < 2:
                        step(V.scalar_tensor_tensor(out=r[:, g], in0=t[:, g], scalar=1.5, in1=r[:, g], op0=ALU.add, op1=ALU.mult))
                    if k == 1:
                        V.scalar_tensor_tensor(out=n[:, g], in0=ms[:, g], scalar=-0.5, in1=r[:, g], op0=ALU.mult, op1=ALU.mult)
                V.scalar_tensor_tensor(out=n[:, g], in0=t[:, g], scalar=1.5, in1=n[:, g], op0=ALU.add, op1=ALU.mult)
                V.scalar_tensor_tensor(out=r[:, g], in0=t[:, g], scalar=1.5, in1=r[:, g],
                                       op0=ALU.add, op1=ALU.mult).then_inc(done, 1)

            def dense(d, edges=None, extra=(), twice=(1,)):
                fixed = d.it is None
                first, second, third = (not fixed or 0 <= d.a - k < NC for k in (0, 2, 4))
                s = d.parity()
                b = s
                if third:
                    dve.wait_ge(s_nt[b], at(counted(d + (-4), 16)))
                    for t in range(1, NT):
                        last = V.tensor_scalar(is_type[t - 1][b][:, :], ntin[b][:, :], t, None, ALU.is_equal)
                if second:
                    dve.wait_ge(s_z, at(d + (-1)) if not fixed else min(d.a - 1, NC))
                    dve.wait_ge(s_x3, at(d + (-2)))
                    last = V.scalar_tensor_tensor(out=y1[:, :, :], in0=flat_bank(pz), scalar=0.0, in1=x1[b][:, :, :],
                                                  op0=ALU.max, op1=ALU.add)
                if third:
                    step(last)
                    dve.wait_ge(s_sel, at(d + (-3)))
                    settle(dve, s_passed)
                    step(V.copy_predicated(sel[b][:, :, :], bc(is_type[0][b][:, :]), flat_bank(po[1])))
                    settle(dve, s_passed)
                    step(V.copy_predicated(sel[b][:, :, :], bc(is_type[1][b][:, :]), flat_bank(po[2])))
                    last = V.scalar_tensor_tensor(out=sel[b][:, :, :], in0=x3[b][:, :, :], scalar=2.0, in1=sel[b][:, :, :],
                                                  op0=ALU.mult, op1=ALU.add)
                elif not second:
                    last = V.memset(tmp[s][0:1, 0:1], 0.0)
                last.then_inc(s_read, 1)
                dve.wait_ge(s_read, at(d + 1))
                if not third:
                    dve.wait_ge(s_x1, min(d.a, NC))
                if first:
                    dve.wait_ge(s_y0, at(d + 1))
                    last = stats(y0[b], s, 2)
                if second:
                    last = stats(y1, s, 1)
                if third:
                    last = stats(sel[b], s, 0)
                if edges:
                    edges()
                for y, g in extra:
                    last = stats(y, s, g)
                step(last)
                lo = 0 if third else 1 if second else 2
                hi = extra[-1][1] + 1 if extra else 3 if first else 2 if second else 1
                rsqrt(s, lo, hi, twice, s_ln)

            def scan(m, k, data0, data1, op0, op1, start=None):
                return V.tensor_tensor_scan(m[:, k, 1:C + 1], data0, data1, m[:, k, 0:1] if start is None else start, op0, op1)

            on_from = lambda m, k: m[:, k, C:C + 1]

            def scores(c):
                b, q = c.parity(), ph[0]
                dve.wait_ge(q["pA"], at(c + 1))
                dve.wait_ge(q["aux"][b], at(counted(c, 64)))
                dve.wait_ge(q["vA"], at(c))
                step(V.tensor_scalar(wc, pc[:, 0:C], 0.2, None, ALU.mult))
                step(V.tensor_tensor(wa, wc, pc[:, 0:C], ALU.max))
                step(scan(run, 0, aux[b][:, :], wa, ALU.add, ALU.max))
                step(V.tensor_tensor(wb, run[:, 0, 0:C], aux[b][:, :], ALU.add))
                V.tensor_tensor(wa, wa, run[:, 0, 1:C + 1], ALU.subtract)
                V.tensor_tensor(wb, wb, run[:, 0, 1:C + 1], ALU.subtract).then_inc(q["vE"], 1)

            def sums(c):
                b, q = c.parity(), ph[0]
                dve.wait_ge(q["eX"], at(c + 1))
                dve.wait_ge(q["pB"], at(c + 1))
                dve.wait_ge(q["dg"][b], at(c.half() * 16))
                dve.wait_ge(q["pR"], at(c))
                V.tensor_tensor_scan(deg[b][:, :], rows_same[b][:, :], one_row,
                                     0.0 if c.it is None and c.a == 0 else deg[1 - b][:, C - 1:C], ALU.mult, ALU.add)
                scan(run, 2, wb, wa, ALU.mult, ALU.add, on_from(run, 2))
                step(V.tensor_tensor(wc, pa[:, 0:C], wa, ALU.mult))
                scan(run, 1, wb, wc, ALU.mult, ALU.add, on_from(run, 1)).then_inc(q["vA"], 1)
                V.tensor_copy(run[:, 0, 0:1], on_from(run, 0))

            def layer0(c):
                b, q = c.parity(), ph[0]
                d0, d1 = dense_of(0, c)
                scores(c)

                def source_rows():
                    dve.wait_ge(q["yb"], at(c + 1))

                def target_rows():
                    dve.wait_ge(q["pR"], at(c + 1))
                    dve.wait_ge(q["yb"], at(c + 1))
                    dve.wait_ge(q["nD"], at(c))
                    dve.wait_ge(q["eN"], at(c + 1))
                    step(V.tensor_scalar(den[:, :], den[:, :], TINY, None, ALU.add))
                    step(V.reciprocal(den[:, :], den[:, :]))
                    step(V.tensor_tensor(yd[:, :, :].rearrange("p j (h k) -> p (j h) k", h=H),
                                         pb[0:R, 0:T * D].rearrange("p (g k) -> p g k", k=HC),
                                         den[:, :].unsqueeze(2).broadcast_to([R, T * H, HC]), ALU.mult))
                    step(V.tensor_tensor(yd[:, :, :], yd[:, :, :], xdb[b][:, :, :], ALU.add))

                dense(d0, source_rows, ((ysb[b], 3),))
                sums(c)
                dense(d1, target_rows, ((yd, 3),))

            def layer1(c):
                b, q = c.parity(), ph[1]
                dve.wait_ge(q["eS"], at(c + 1))
                dve.wait_ge(q["aux"][b], at(counted(c, 48)))
                dve.wait_ge(q["pR"], at(c))
                step(scan(run, 0, same[b][:, :], stf, ALU.mult, ALU.add, on_from(run, 0)))
                V.tensor_tensor(aggf, run[:, 0, 1:C + 1], aux[b][:, :], ALU.mult).then_inc(q["vA"], 1)

                def edge_rows():
                    dve.wait_ge(q["pR"], at(c + 1))
                    dve.wait_ge(q["nS"], at(c))
                    dve.wait_ge(q["nD"], at(c))
                    V.scalar_tensor_tensor(out=ys[:, :, :], in0=flat_bank(pa), scalar=0.0, in1=xs[b][:, :, :],
                                           op0=ALU.max, op1=ALU.add)
                    V.scalar_tensor_tensor(out=yd[:, :, :], in0=flat_bank(pb), scalar=0.0, in1=xd[b][:, :, :],
                                           op0=ALU.max, op1=ALU.add).then_inc(q["rd"], 1)
                    dve.wait_ge(q["rd"], at(c + 1))

                dense(dense_of(1, c)[0], edge_rows, ((ys, 3), (ys, 4), (yd, 5)), (1, 4))

            def masks(c):
                b, q = c.parity(), ph[2]
                dve.wait_ge(q["eS"], at(c + 1))
                dve.wait_ge(q["rl"][b], at(counted(c, 16)))
                dve.wait_ge(q["pM"], at(c * REL))
                for r in range(REL):
                    V.scalar_tensor_tensor(out=masked[:, r, :], in0=rel[b][:, :], scalar=float(r), in1=stf,
                                           op0=ALU.is_equal, op1=ALU.mult).then_inc(q["vM"], 1)

            def layer2(c):
                b, q = c.parity(), ph[2]
                dve.wait_ge(q["aux"][b], at(counted(c, 32)))
                dve.wait_ge(q["pM"], at((c + 1) * REL))
                dve.wait_ge(q["pR"], at(c))
                scan(run, 0, same[b][:, :], pb[:, 0:C], ALU.mult, ALU.add, on_from(run, 0)).then_inc(q["vA"], 1)
                if there(c + 1):
                    masks(c + 1)

                def target_rows():
                    dve.wait_ge(q["pR"], at(c + 1))
                    dve.wait_ge(q["nD"], at(c))
                    step(V.tensor_tensor(yd[:, :, :], xd[b][:, :, :], flat_bank(pa), ALU.add))

                dense(dense_of(2, c)[0], target_rows, ((yd, 3),))

            def message_sums(c):
                b, q = c.parity(), ph[3]
                m, before = (run, run2) if b == 0 else (run2, run)
                dve.wait_ge(q["aux"][b], at(counted(c, 32)))
                dve.wait_ge(q["pR"], at(c + (-1)))
                for t in range(NT):
                    dve.wait_ge(q["eX"], at(c * NT + (t + 1)))
                    scan(m, t, same[b][:, :], masked[:, t, :], ALU.mult, ALU.add,
                         before[:, t, C:C + 1]).then_inc(q["vA"], 1)

            def updated_rows(c):
                b, q = c.parity(), ph[3]
                for t in range(1, NT):
                    last = V.tensor_scalar(is_type[t - 1][0][:, :], ntd_all[:, c.v(), :], t, None, ALU.is_equal)
                step(last)
                dve.wait_ge(q["sel"], at(c + 1))
                settle(dve, s_passed)
                step(V.copy_predicated(ys[:, :, :], bc(is_type[0][0][:, :]), flat_bank(bank[6])))
                settle(dve, s_passed)
                step(V.copy_predicated(ys[:, :, :], bc(is_type[1][0][:, :]), flat_bank(bank[7])))
                dve.wait_ge(q["nD"], at(c))
                V.scalar_tensor_tensor(out=yd[:, :, :], in0=xd[b][:, :, :], scalar=2.0, in1=ys[:, :, :],
                                       op0=ALU.mult, op1=ALU.add).then_inc(q["rd"], 1)
                dve.wait_ge(q["rd"], at(c + 1))
                step(stats(yd, b, 3))
                rsqrt(b, 3, 4, (), q["vN"])

            def layer3(c):
                if c.it is not None or c.a >= 1:
                    updated_rows(c + (-1))
                if there(c + 1):
                    message_sums(c + 1)

            over(dve, layer0, chain, DVE_STEPS[0])
            dve.wait_ge(s_rdeg, 16)
            V.reciprocal(degp[:, :], degp[:, :]).then_inc(s_rd, 1)
            step(V.memset(run[:, 0, C:C + 1], 0.0))
            over(dve, layer1, chain, DVE_STEPS[1])
            step(V.memset(run[:, 0, C:C + 1], 0.0))
            masks(Lin(0))
            over(dve, layer2, chain, DVE_STEPS[2])
            for d in range(NC, NC + 4):
                dense(Lin(d))
            step(V.memset(run2[:, :, C:C + 1], 0.0))
            message_sums(Lin(0))
            over(dve, layer3, chain, DVE_STEPS[3])
            updated_rows(Lin(EC - 1))

        @block.scalar
        def _(act):
            A = nc.scalar.activation

            def normalize(to, y, s, g):
                for j in range(T):
                    k = g * T + j
                    last = A(to[:, j, :], y[:, j, :], ACT.Identity, scale=rst[s][:, k:k + 1], bias=nmr[s][:, k:k + 1])
                return last

            def dense(d, edges=None):
                fixed = d.it is None
                first, second, third = (not fixed or 0 <= d.a - k < NC for k in (0, 2, 4))
                s = d.parity()
                if not fixed or 0 <= d.a - 3 < NC:
                    act.wait_ge(s_o, at(d + (-2)))
                    if not fixed or d.a > 4:
                        act.wait_ge(s_out, at(d + (-4)))
                    A(sel[1 - s][:, :, :], flat_bank(po[0]), ACT.Copy).then_inc(s_sel, 1)
                act.wait_ge(s_ln, at(d + 1))
                if second:
                    normalize(x3[s], y1, s, 1).then_inc(s_x3, 1)
                if first:
                    normalize(x1[s], y0[s], s, 2).then_inc(s_x1, 1)
                if second:
                    act.wait_ge(s_tr, at(d + (-1)))
                    A(rt[:, :, :], by_tile(pt), ACT.Relu).then_inc(s_rt, 1)
                if third:
                    act.wait_ge(s_res[s], at((d + (-4)).half() * 16))
                    normalize(res[s], sel[s], s, 0).then_inc(s_out, 1)
                if first:
                    act.wait_ge(s_tx, at(d + 1))
                    A(xt[:, :, :], by_tile(pt), ACT.Copy).then_inc(s_xt, 1)
                if edges:
                    edges()

            natural = lambda a: a[:, :, :].rearrange("d p j -> d j p")

            def evacuate_sources(c, p, k):
                q = ph[p]
                act.wait_ge(q["tS"], at(c + 1))
                A(natural(st), by_tile(bank[k]), ACT.Copy).then_inc(q["eS"], 1)

            def evacuate_targets(c, p, k, to, func):
                q = ph[p]
                act.wait_ge(q["tD"], at(c + 1))
                A(natural(to), by_tile(bank[k]), func).then_inc(q["eD"], 1)

            def layer0(c):
                b, q = c.parity(), ph[0]
                d0, d1 = dense_of(0, c)
                act.wait_ge(q["vE"], at(c + 1))
                A(wb, wb, ACT.Exp)
                A(wa, wa, ACT.Exp).then_inc(q["eX"], 1)

                def source_rows():
                    act.wait_ge(q["stS"][b], at(c.half() * 16))
                    normalize(so[b], ysb[b], 0, 3).then_inc(q["nS"], 1)

                def target_rows():
                    act.wait_ge(q["stD"][b], at(c.half() * 16))
                    normalize(do[b], yd, 1, 3).then_inc(q["nD"], 1)

                dense(d0, source_rows)
                act.wait_ge(q["pR"], at(c + 1))
                act.wait_ge(s_ln, at(d0 + 1))
                A(den[:, 0:3 * H], pc[0:R, C:C + 3 * H], ACT.Copy)
                A(den[:, 3 * H:4 * H], pa[0:R, C:C + H], ACT.Copy).then_inc(q["eN"], 1)
                if there(c + 1):
                    evacuate_sources(c + 1, 0, 5)
                    evacuate_targets(c + 1, 0, 5, dt, ACT.Copy)
                dense(d1, target_rows)

            def layer1(c):
                b, q = c.parity(), ph[1]
                s = block_of(1, c).parity()
                if there(c + 1):
                    evacuate_sources(c + 1, 1, 7)
                    evacuate_targets(c + 1, 1, 7, dt, ACT.Copy)

                def edge_rows():
                    act.wait_ge(q["stS"][b], at(c.half() * 32))
                    normalize(so[b], ys, s, 3)
                    normalize(so3[b], ys, s, 4).then_inc(q["nS"], 1)
                    act.wait_ge(q["stD"][b], at(c.half() * 16))
                    normalize(do[b], yd, s, 5).then_inc(q["nD"], 1)

                dense(dense_of(1, c)[0], edge_rows)

            def layer2(c):
                b, q = c.parity(), ph[2]
                s = block_of(2, c).parity()
                if there(c + 2):
                    act.wait_ge(q["vM"], at((c + 2) * REL))
                    evacuate_sources(c + 2, 2, 7)

                def target_rows():
                    act.wait_ge(q["stD"][b], at(c.half() * 16))
                    normalize(do[b], yd, s, 3).then_inc(q["nD"], 1)

                dense(dense_of(2, c)[0], target_rows)

            def messages(c):
                b, q = c.parity(), ph[3]
                evacuate_sources(c, 3, 0)
                for t in range(NT):
                    act.wait_ge(q["pM"], at(c * NT + (t + 1)))
                    act.wait_ge(q["vA"], at(c * NT))
                    A(masked[:, t, :], bank[2 + t][:, 0:C], ACT.Relu, bias=bet[:, t:t + 1]).then_inc(q["eX"], 1)
                act.wait_ge(q["pR"], at(c + (-1)))
                evacuate_targets(c, 3, 1, (dt, agg)[b], ACT.Relu)

            def products_of_type(c):
                q = ph[3]
                act.wait_ge(q["pR"], at(c + 1))
                act.wait_ge(q["rd"], at(c))
                A(ys[:, :, :], flat_bank(bank[5]), ACT.Copy).then_inc(q["sel"], 1)

            def results(c):
                b, q = c.parity(), ph[3]
                act.wait_ge(q["vN"], at(c + 1))
                act.wait_ge(q["sc"][b], at(c.half() * (16 * T)))
                normalize(do[b], yd, b, 3).then_inc(q["nD"], 1)

            def layer3(c):
                before = c.it is not None or c.a >= 1
                if before:
                    products_of_type(c + (-1))
                if there(c + 1):
                    messages(c + 1)
                if before:
                    results(c + (-1))

            act.wait_ge(s_w, 16 * NLOADS)
            evacuate_sources(Lin(0), 0, 5)
            evacuate_targets(Lin(0), 0, 5, dt, ACT.Copy)
            over(act, layer0)
            evacuate_sources(Lin(0), 1, 7)
            evacuate_targets(Lin(0), 1, 7, dt, ACT.Copy)
            over(act, layer1)
            evacuate_sources(Lin(0), 2, 7)
            act.wait_ge(ph[2]["vM"], REL)
            evacuate_sources(Lin(1), 2, 7)
            over(act, layer2)
            for d in range(NC, NC + 4):
                dense(Lin(d))
            messages(Lin(0))
            over(act, layer3)
            products_of_type(Lin(EC - 1))
            results(Lin(EC - 1))

        @block.tensor
        def _(pe):
            mm = nc.tensor.matmul

            def turn(to, rows_):
                for j in range(T):
                    last = nc.tensor.transpose(tile_of(to, j), rows_[:, j, :], ident[0:R, 0:R])
                return last

            def biased(to, i):
                mm(to[0:R, 0:T * D], ones_bf[:, 0:R], bparts[:, i, :, :].rearrange("k j d -> k (j d)"), start=True, stop=False, skip_group_check=True)

            def product(to, left, right, stop=True):
                for j in range(T):
                    last = mm(to[0:R, j * D:(j + 1) * D], left(j), right, start=False, stop=stop and j == T - 1, skip_group_check=True)
                return last

            pe.wait_ge(s_w, 16 * NLOADS)
            pe.wait_ge(s_bp, 1)
            for k in range(2):
                mm(bank[0][:, 0:D], b1m[:, k, :], w2[:, k, :], start=k == 0, stop=k == 1)
            for a in range(2):
                for k in range(2):
                    last = mm(bank[1][:, a * D:(a + 1) * D], w1t[:, k, a * D:(a + 1) * D], w2[:, k, :], start=k == 0, stop=k == 1)
            last.then_inc(s_pe0, 1)
            pe.wait_ge(s_bp, 2)
            pe.wait_ge(s_pchain, 1)

            pe.wait_ge(s_hs, 1)

            def dense_turns(d):
                fixed = d.it is None
                first, second = (not fixed or 0 <= d.a - k < NC for k in (0, 2))
                if second:
                    pe.wait_ge(s_x3, at(d + (-1)))
                    pe.wait_ge(s_xt, at(d) if not fixed else min(d.a, NC))
                    turn(pt, x3[d.parity()]).then_inc(s_tr, 1)
                if first:
                    pe.wait_ge(s_x1, at(d + 1))
                    if second:
                        pe.wait_ge(s_rt, at(d + (-1)))
                    else:
                        pe.wait_ge(s_xt, at(d))
                    turn(pt, x1[d.parity()]).then_inc(s_tx, 1)

            def dense_products(d):
                fixed = d.it is None
                first, second = (not fixed or 0 <= d.a - k < NC for k in (0, 2))
                if first or second:
                    pe.wait_ge(s_read, at(d + 2))
                if second:
                    pe.wait_ge(s_rt, at(d + (-1)))
                    for t in range(NT):
                        biased(po[t], 2 + t)
                        last = product(po[t], lambda j: rt[:, j, :], wnt[:, 0, t, :])
                    last.then_inc(s_o, 1)
                if first:
                    pe.wait_ge(s_xt, at(d + 1))
                    biased(pz, 0)
                    product(pz, lambda j: xt[:, j, :], wab[:, 0, :]).then_inc(s_z, 1)

            def dense(d):
                dense_products(d + (-1))
                dense_turns(d)

            def front0(c):
                b, q = c.parity(), ph[0]
                pe.wait_ge(q["g"][b], at(counted(c, 32 * T)))
                pe.wait_ge(q["vA"], at(c))
                pe.wait_ge(q["eN"], at(c))
                turn(pa, xs[b]).then_inc(q["tS"], 1)
                pe.wait_ge(q["eS"], at(c + 1))
                turn(pa, xd[b]).then_inc(q["tD"], 1)
                pe.wait_ge(q["aux"][b], at(counted(c, 64)))
                pe.wait_ge(q["vE"], at(c))
                mm(pc[:, 0:C], ks[:, :], stf, start=True, stop=False)
                mm(pc[:, 0:C], es[:, :], ea[b][:, :], start=False, stop=False)
                pe.wait_ge(q["eD"], at(c + 1))
                mm(pc[:, 0:C], qs[:, :], dtf, start=False, stop=True).then_inc(q["pA"], 1)
                mm(pa[:, 0:C], wv[:, :], stf, start=True, stop=True).then_inc(q["pB"], 1)

            def layer0(c):
                b, q = c.parity(), ph[0]
                d0, d1 = dense_of(0, c)
                dense(d0)
                pe.wait_ge(q["vA"], at(c + 1))
                for j in range(T):
                    mm(pb[0:R, j * D:(j + 1) * D], run_tile(run, 1, j), ident[:, :], start=True, stop=True)
                for j in range(T):
                    to = pc[0:R, C + j * H:C + (j + 1) * H] if j < T - 1 else pa[0:R, C:C + H]
                    last = mm(to, run_tile(run, 2, j), headsel[:, :], start=True, stop=True)
                last.then_inc(q["pR"], 1)
                if there(c + 1):
                    front0(c + 1)
                dense(d1)

            def turns1(c):
                b, q = c.parity(), ph[1]
                pe.wait_ge(q["g"][b], at(counted(c, 16 * T)))
                pe.wait_ge(q["aux"][b], at(counted(c, 48)))
                turn(pc, xs[b]).then_inc(q["tS"], 1)
                pe.wait_ge(q["eS"], at(c + 1))
                turn(pc, xd[b]).then_inc(q["tD"], 1)

            def products1(c):
                q = ph[1]
                pe.wait_ge(q["rd"], at(c))
                pe.wait_ge(q["eS"], at(c + 1))
                biased(pa, 0)
                product(pa, lambda j: st[:, :, j], wab[:, 0, :])
                pe.wait_ge(q["eD"], at(c + 1))
                biased(pb, 0)
                product(pb, lambda j: dt[:, :, j], wab[:, 0, :], stop=False)

            def layer1(c):
                q = ph[1]
                pe.wait_ge(q["vA"], at(c + 1))
                product(pb, lambda j: agg[:, :, j], wab[:, 1, :]).then_inc(q["pR"], 1)
                if there(c + 1):
                    turns1(c + 1)
                d = dense_of(1, c)[0]
                dense_products(d + (-1))
                if there(c + 1):
                    products1(c + 1)
                dense_turns(d)

            def turns2(c):
                b, q = c.parity(), ph[2]
                pe.wait_ge(q["g"][b], at(counted(c, 16 * T)))
                pe.wait_ge(q["eS"], at(c))
                turn(pc, xs[b]).then_inc(q["tS"], 1)

            def relations2(c):
                q = ph[2]
                pe.wait_ge(q["vA"], at(c))
                for r in range(REL):
                    pe.wait_ge(q["vM"], at(c * REL + (r + 1)))
                    mm(pb[:, 0:C], wr[:, r, :], masked[:, r, :], start=r == 0, stop=r == REL - 1).then_inc(q["pM"], 1)

            def layer2(c):
                q = ph[2]
                pe.wait_ge(q["vA"], at(c + 1))
                if c.it is not None or c.a >= 1:
                    pe.wait_ge(s_ln, at(block_of(2, c)))
                for j in range(T):
                    last = mm(pa[0:R, j * D:(j + 1) * D], run_tile(run, 0, j), ident[:, :], start=True, stop=True)
                last.then_inc(q["pR"], 1)
                if there(c + 1):
                    relations2(c + 1)
                if there(c + 2):
                    turns2(c + 2)
                dense(dense_of(2, c)[0])

            def messages(c):
                b, q = c.parity(), ph[3]
                pe.wait_ge(q["g"][b], at(counted(c, 16 * T)))
                pe.wait_ge(q["ld"][b], at(counted(c, 32)))
                pe.wait_ge(q["eS"], at(c))
                turn(bank[0], xs[b]).then_inc(q["tS"], 1)
                pe.wait_ge(q["eS"], at(c + 1))
                pe.wait_ge(q["eX"], at(c * NT))
                for t in range(NT):
                    mm(bank[2 + t][:, 0:C], ones_bf[0:1, :], off[b][0:1, t, :], start=True, stop=False)
                    mm(bank[2 + t][:, 0:C], wet[:, t, :], stf, start=False, stop=True).then_inc(q["pM"], 1)

            def targets(c):
                b, q = c.parity(), ph[3]
                pe.wait_ge(q["aux"][b], at(counted(c, 32)))
                pe.wait_ge(q["eD"], at(c))
                turn(bank[1], xd[b]).then_inc(q["tD"], 1)

            def layer3(c):
                b, q = c.parity(), ph[3]
                if there(c + 1):
                    messages(c + 1)
                pe.wait_ge(q["eD"], at(c + 1))
                pe.wait_ge(q["rd"], at(c))
                own, sums = (dt, agg)[b], (run, run2)[b]
                for t in range(NT):
                    biased(bank[5 + t], 2 + t)
                    product(bank[5 + t], lambda j: own[:, :, j], wnt[:, 0, t, :], stop=False)
                if there(c + 1):
                    targets(c + 1)
                for k in range(NT):
                    pe.wait_ge(q["vA"], at(c * NT + (k + 1)))
                    for t in range(NT):
                        last = product(bank[5 + t], lambda j: run_tile(sums, k, j), wnt[:, 1 + k, t, :], stop=k == NT - 1)
                last.then_inc(q["pR"], 1)

            front0(Lin(0))
            over(pe, layer0)
            turns1(Lin(0))
            products1(Lin(0))
            over(pe, layer1)
            turns2(Lin(0))
            relations2(Lin(0))
            turns2(Lin(1))
            over(pe, layer2)
            for d in range(NC, NC + 4):
                dense(Lin(d))
            messages(Lin(0))
            targets(Lin(0))
            over(pe, layer3)


def kernel(**inputs):
    import numpy as np
    import concourse.bacc as bacc
    from concourse.bass_utils import run_bass_kernel_spmd

    a = {k: np.asarray(v) for k, v in inputs.items()}
    W1, W2 = a["L1_gnn_W1"], a["L1_gnn_W2"]
    n, t = a["x"].shape[0], a["L3_gnn_W_e"].shape[0]
    laid = {
        "x": a["x"], "src": a["src"], "dst": a["dst"], "eattrT": a["edge_attr_64"].T,
        "etype3": a["edge_type_3"], "etype8": a["edge_type_8"][None], "eweight": a["edge_weight"][None],
        "ntype3": a["node_type_3"][:, None], "Wq": a["L0_gnn_Wq"], "Wk": a["L0_gnn_Wk"], "Wv": a["L0_gnn_Wv"],
        "We": a["L0_gnn_We"], "gate": a["L0_gnn_gate"], "bias0": a["L0_gnn_bias"][None],
        "W1T": W1.T.reshape(2, D, 2 * D).transpose(1, 0, 2), "b1": a["L1_gnn_b1"].reshape(2, D).T,
        "W2": W2.reshape(2, D, D).transpose(1, 0, 2), "b2": a["L1_gnn_b2"][None],
        "Wr": a["L2_gnn_weight"].transpose(1, 0, 2), "WeT": a["L3_gnn_W_e"].transpose(2, 0, 1),
        "beT": a["L3_gnn_b_e"].T, "WnT": a["L3_gnn_W_n"].reshape(t, D, 1 + t, D).transpose(3, 2, 0, 1),
        "bn": a["L3_gnn_b_n"], "ident": np.eye(D, dtype=np.float32),
    }
    nc = bacc.Bacc("TRN2", target_bir_lowering=False, num_devices=1)
    arrays, args = {}, []
    for name, v in laid.items():
        v = np.ascontiguousarray(v)
        arrays[f"in_{name}"] = v
        args.append(nc.dram_tensor(f"in_{name}", v.shape, mybir.dt.from_np(v.dtype), kind="ExternalInput").ap())
    args.append(nc.dram_tensor("out_rows", [n, D], F32, kind="ExternalOutput").ap())
    gnn_kernel(nc, *args)
    r = run_bass_kernel_spmd(nc, [arrays], core_ids=[0])
    return r.results[0]["out_rows"]
```
